# Optimizing a Trainium2 kernel written in Bass

```python
import numpy as np
import jax
import jax.numpy as jnp

def _softmax(x, axis=-1):
    return jax.nn.softmax(x, axis=axis)

def _gelu(x):
    return jax.nn.gelu(x, approximate=True)

def _silu(x):
    return jax.nn.silu(x)

def _sigmoid(x):
    return jax.nn.sigmoid(x)

def _layernorm(x, axis=-1, eps=1e-05):
    m = jnp.mean(x, axis=axis, keepdims=True)
    v = jnp.var(x, axis=axis, keepdims=True)
    return (x - m) / jnp.sqrt(v + eps)

def _scatter_add(tgt, idx, src, axis=0):
    return tgt.at[idx].add(src)

def _segment_sum(src, seg, n):
    return jax.ops.segment_sum(src, seg, n)
kernel_name = 'mk_adj_preln_d4_adj_r2_e691f3'

def setup_inputs(seed: int=0):
    np.random.seed(seed)
    _w = jnp.asarray

    def _rec_inputs():
        import jax
        import jax.numpy as jnp
        _gk = jax.random.key(seed)
        x = -0.000125 + 0.9999 * jax.random.normal(jax.random.fold_in(_gk, 1), (64, 128, 256), jnp.float32)
        _w = (1.0 + jnp.arange(128, dtype=jnp.float32)) ** (-0.5)
        _w = _w / _w.mean()
        _pij = jnp.clip(0.03125 * _w[:, None] * _w[None, :], 0.0, 1.0)
        _a = jax.random.uniform(jax.random.fold_in(_gk, 2), (128, 128)) < _pij
        _af = _a.astype(jnp.float32)
        adj = _af
        return (x, adj)
    x, adj = _rec_inputs()

    def _L0_gnn_setup():
        import jax, jax.numpy as jnp
        import numpy as np
        ALPHA = 0.2
        key = jax.random.key(seed)
        k0, k1, k2, k3 = jax.random.split(key, 4)
        B, N, C, F = (64, 512, 256, 256)
        x = jax.random.normal(k0, (B, N, C), dtype=jnp.float32)
        W = jax.random.normal(k1, (C, F), dtype=jnp.float32) * (1.414 / np.sqrt(C + F))
        a = jax.random.normal(k2, (2 * F, 1), dtype=jnp.float32) * (1.414 / np.sqrt(2 * F + 1))
        beta = jnp.ones((1,), dtype=jnp.float32)
        mask = (jax.random.uniform(k3, (N, N)) < 0.3).astype(jnp.float32)
        return {'x': x, 'W': W, 'a': a, 'beta': beta, 'mask': mask}
    _L0_gnn_all = _L0_gnn_setup()
    _L0_gnn_in = {k: v for k, v in _L0_gnn_all.items() if k in ('W', 'a', 'beta')}
    del _L0_gnn_all

    def _L1_gnn_setup():
        import jax, jax.numpy as jnp
        import numpy as np
        B, N, F_IN, F_OUT = (16, 1024, 256, 256)
        key = jax.random.key(seed)
        k1, k2, k3 = jax.random.split(key, 3)
        x = jax.random.normal(k1, (B, N, F_IN), dtype=jnp.float32)
        adj = jax.random.uniform(k2, (N, N), dtype=jnp.float32)
        bound = np.sqrt(6.0 / F_OUT)
        weight = jax.random.uniform(k3, (F_IN, F_OUT), dtype=jnp.float32, minval=-bound, maxval=bound)
        bias = jnp.zeros((F_OUT,), dtype=jnp.float32)
        return {'x': x, 'adj': adj, 'weight': weight, 'bias': bias}
    _L1_gnn_all = _L1_gnn_setup()
    _L1_gnn_in = {k: v for k, v in _L1_gnn_all.items() if k in ('weight', 'bias')}
    del _L1_gnn_all

    def _L2_gnn_setup():
        import jax, jax.numpy as jnp
        import numpy as np
        B, N, D, T = (64, 128, 256, 3)

        def _lin(v, W, b):
            return jnp.einsum('...i,oi->...o', v, W) + b
        key = jax.random.key(seed)
        ks = jax.random.split(key, 12)
        s2 = 1.0 / np.sqrt(2 * D)
        s1 = 1.0 / np.sqrt(D)
        return {'x': jax.random.normal(ks[0], (B, N, D), jnp.float32), 'in_mat': jax.random.uniform(ks[1], (N, N), jnp.float32) / N, 'out_mat': jax.random.uniform(ks[2], (N, N), jnp.float32) / N, 'w3_w': jax.random.normal(ks[3], (D, 2 * D), jnp.float32) * s2, 'w3_b': jnp.zeros((D,), jnp.float32), 'u3_w': jax.random.normal(ks[4], (D, D), jnp.float32) * s1, 'u3_b': jnp.zeros((D,), jnp.float32), 'w4_w': jax.random.normal(ks[5], (D, 2 * D), jnp.float32) * s2, 'w4_b': jnp.zeros((D,), jnp.float32), 'w5_w': jax.random.normal(ks[6], (D, 2 * D), jnp.float32) * s2, 'w5_b': jnp.zeros((D,), jnp.float32), 'u5_w': jax.random.normal(ks[7], (D, D), jnp.float32) * s1, 'u5_b': jnp.zeros((D,), jnp.float32)}
    _L2_gnn_all = _L2_gnn_setup()
    _L2_gnn_in = {k: v for k, v in _L2_gnn_all.items() if k in ('w3_w', 'w3_b', 'u3_w', 'u3_b', 'w4_w', 'w4_b', 'w5_w', 'w5_b', 'u5_w', 'u5_b')}
    del _L2_gnn_all

    def _L3_gnn_setup():
        import jax, jax.numpy as jnp
        import numpy as np
        B, N, D, O = (8, 2048, 256, 256)
        key = jax.random.key(seed)
        k1, k2, k3, k4 = jax.random.split(key, 4)
        x = jax.random.normal(k1, (B, N, D), dtype=jnp.float32)
        adj = jax.random.uniform(k2, (N, N), dtype=jnp.float32)
        weight = jax.random.normal(k3, (D, O), dtype=jnp.float32) * 0.02
        bias = jax.random.normal(k4, (O,), dtype=jnp.float32) * 0.02
        return {'x': x, 'adj': adj, 'weight': weight, 'bias': bias}
    _L3_gnn_all = _L3_gnn_setup()
    _L3_gnn_in = {k: v for k, v in _L3_gnn_all.items() if k in ('weight', 'bias')}
    del _L3_gnn_all
    return {'x': x, 'adj': adj, 'L0_gnn_W': _L0_gnn_in['W'], 'L0_gnn_a': _L0_gnn_in['a'], 'L0_gnn_beta': _L0_gnn_in['beta'], 'L1_gnn_weight': _L1_gnn_in['weight'], 'L1_gnn_bias': _L1_gnn_in['bias'], 'L2_gnn_w3_w': _L2_gnn_in['w3_w'], 'L2_gnn_w3_b': _L2_gnn_in['w3_b'], 'L2_gnn_u3_w': _L2_gnn_in['u3_w'], 'L2_gnn_u3_b': _L2_gnn_in['u3_b'], 'L2_gnn_w4_w': _L2_gnn_in['w4_w'], 'L2_gnn_w4_b': _L2_gnn_in['w4_b'], 'L2_gnn_w5_w': _L2_gnn_in['w5_w'], 'L2_gnn_w5_b': _L2_gnn_in['w5_b'], 'L2_gnn_u5_w': _L2_gnn_in['u5_w'], 'L2_gnn_u5_b': _L2_gnn_in['u5_b'], 'L3_gnn_weight': _L3_gnn_in['weight'], 'L3_gnn_bias': _L3_gnn_in['bias']}

def reference(x, adj, L0_gnn_W, L0_gnn_a, L0_gnn_beta, L1_gnn_weight, L1_gnn_bias, L2_gnn_w3_w, L2_gnn_w3_b, L2_gnn_u3_w, L2_gnn_u3_b, L2_gnn_w4_w, L2_gnn_w4_b, L2_gnn_w5_w, L2_gnn_w5_b, L2_gnn_u5_w, L2_gnn_u5_b, L3_gnn_weight, L3_gnn_bias):
    import jax
    import jax.numpy as jnp

    def _L0_gnn_ref(x, W, a, beta, mask):
        import jax, jax.numpy as jnp
        import numpy as np
        ALPHA = 0.2
        F_ = W.shape[1]
        h = jnp.einsum('bnc,cf->bnf', x, W)
        a1, a2 = (a[:F_, 0], a[F_:, 0])
        s1 = jnp.einsum('bnf,f->bn', h, a1)
        s2 = jnp.einsum('bnf,f->bn', h, a2)
        e = jax.nn.leaky_relu(s1[:, :, None] + s2[:, None, :], negative_slope=ALPHA)
        e = e * mask[None, :, :]
        att = jax.nn.softmax(e, axis=2)
        h_prime = jnp.einsum('bij,bjf->bif', att, h)
        return jax.nn.elu(h_prime + beta * h)

    def _L1_gnn_ref(x, adj, weight, bias):
        import jax, jax.numpy as jnp
        import numpy as np
        B, N, F_IN, F_OUT = (16, 1024, 256, 256)
        deg = adj.sum(axis=1)
        deg_inv_sqrt = jnp.where(deg > 0, jax.lax.rsqrt(deg), 0.0)
        norm_adj = adj * deg_inv_sqrt[:, None] * deg_inv_sqrt[None, :]
        support = jnp.einsum('bni,io->bno', x, weight)
        output = jnp.einsum('nm,bmo->bno', norm_adj, support)
        return output + bias

    def _L2_gnn_ref(x, in_mat, out_mat, w3_w, w3_b, u3_w, u3_b, w4_w, w4_b, w5_w, w5_b, u5_w, u5_b):
        import jax, jax.numpy as jnp
        import numpy as np
        B, N, D, T = (64, 128, 256, 3)

        def _lin(v, W, b):
            return jnp.einsum('...i,oi->...o', v, W) + b
        h = x
        for _ in range(T):
            a_in = jnp.einsum('nm,bmd->bnd', in_mat, h)
            a_out = jnp.einsum('nm,bmd->bnd', out_mat, h)
            av = jnp.concatenate([a_in, a_out], axis=-1)
            z = jax.nn.sigmoid(_lin(av, w3_w, w3_b) + _lin(h, u3_w, u3_b))
            r = jax.nn.sigmoid(_lin(av, w4_w, w4_b) + _lin(h, u3_w, u3_b))
            hv = jnp.tanh(_lin(av, w5_w, w5_b) + _lin(r * h, u5_w, u5_b))
            h = (1.0 - z) * h + z * hv
        return h

    def _L3_gnn_ref(x, adj, weight, bias):
        import jax, jax.numpy as jnp
        import numpy as np
        B, N, D, O = (8, 2048, 256, 256)
        y = jnp.einsum('nm,bmd->bnd', adj, x)
        out = jnp.einsum('bnd,do->bno', y, weight) + bias
        return out
    h = jnp.maximum(_layernorm(x, axis=-1), 0.0)
    x = x + _L0_gnn_ref(h, L0_gnn_W, L0_gnn_a, L0_gnn_beta, adj)
    h = jnp.maximum(_layernorm(x, axis=-1), 0.0)
    x = x + _L1_gnn_ref(h, adj, L1_gnn_weight, L1_gnn_bias)
    h = jnp.maximum(_layernorm(x, axis=-1), 0.0)
    x = x + _L2_gnn_ref(h, adj, adj, L2_gnn_w3_w, L2_gnn_w3_b, L2_gnn_u3_w, L2_gnn_u3_b, L2_gnn_w4_w, L2_gnn_w4_b, L2_gnn_w5_w, L2_gnn_w5_b, L2_gnn_u5_w, L2_gnn_u5_b)
    h = jnp.maximum(_layernorm(x, axis=-1), 0.0)
    x = x + _L3_gnn_ref(h, adj, L3_gnn_weight, L3_gnn_bias)
    return x

_drawn_inputs = setup_inputs


def setup_inputs(seed=0):
    import zlib

    import numpy as np

    out = dict(_drawn_inputs(seed))
    spreads = {'L1_gnn_bias': (0.0, 0.1),
     'L2_gnn_w3_b': (0.0, 0.446),
     'L2_gnn_u3_b': (0.0, 0.441),
     'L2_gnn_w4_b': (0.0, 2.0),
     'L2_gnn_w5_b': (0.0, 0.1),
     'L2_gnn_u5_b': (0.0, 0.1)}
    factors = {'L0_gnn_a': 6.083, 'L3_gnn_bias': 6.585}
    for name, (base, spread) in spreads.items():
        noise = np.random.default_rng([zlib.crc32(name.encode()), seed]).standard_normal(out[name].shape)
        drawn = base * np.exp(spread * noise) if base else spread * noise
        out[name] = jnp.asarray(drawn.astype(out[name].dtype))
    for name, factor in factors.items():
        out[name] = (out[name] * factor).astype(out[name].dtype)
    return out
```

```python
import concourse.bass as bass
from concourse import mybir
from contextlib import ExitStack

F32 = mybir.dt.float32
F32R = mybir.dt.float32r
ALU = mybir.AluOpType
ACT = mybir.ActivationFunctionType
AX = mybir.AxisListType

P = 128
C = 256
KB = C // P
B = 64
GB = 4
NS = 2
NG = B // GB // NS
W = GB * P
T = 3
EPS = 1e-5
SLOPE = 0.2
TINY = 1.1754943508222875e-38

STAGES = (
    ["ln0", "turn0", "scores", "project0", "softmax", "turn_p", "attend"]
    + ["ln1", "spread1", "mix1", "ln2", "turn2"]
    + [f"{name}{t}" for t in range(T) for name in (["back"] if t else []) + ["u", "a", "z", "v", "r", "c"]]
    + ["back3", "ln3", "spread3", "mix3"]
)
LAG = len(STAGES) // 2
HEAD = [(0, 0, s) for s in STAGES[:LAG]]
BODY = []
for n in range(len(STAGES)):
    BODY.append((1, 0, STAGES[n]))
    m = n + LAG
    BODY.append((0, m // len(STAGES), STAGES[m % len(STAGES)]))
TAIL = [x for x in BODY if x[1] == 0]


def split(stage):
    return stage.rstrip("0123456789"), int("0" + stage[len(stage.rstrip("0123456789")):])


class Signal:

    def __init__(self, ctx, nc, name, per_group):
        self.sem = [ctx.enter_context(nc.semaphore(f"{name}_{s}")) for s in range(NS)]
        self.per_group = per_group

    def count(self, g, n):
        return g * self.per_group + n


def build(nc, x, adj, adjT, ident_in, w0, w0T, a_cols, beta, w1, b1, w3T, w4T, w5T, u3T, u5T, gate_b, wl, bl, out):
    with ExitStack() as ctx:
        def sb(name, shape, dt=F32):
            return ctx.enter_context(nc.sbuf_tensor(name, shape, dt))

        def sem(name):
            return ctx.enter_context(nc.semaphore(name))

        def signal(name, per_group):
            return Signal(ctx, nc, name, per_group)

        def per_stream(name, shape, dt=F32):
            return [sb(f"{name}_{s}", shape, dt) for s in range(NS)]

        A = sb("A", [P, P])
        AT = sb("AT", [P, P])
        NT = sb("NT", [P, P])
        ident = sb("ident", [P, P])
        betaI = sb("betaI", [P, P])
        W0 = sb("W0", [P, KB, C])
        W0T = sb("W0T", [P, KB, C])
        W1 = sb("W1", [P, KB, C])
        WL = sb("WL", [P, KB, C])
        B1 = sb("B1", [P, C])
        BL = sb("BL", [P, C])
        acol = sb("acol", [P, 2 * KB])
        a2bc = sb("a2bc", [P, KB, P])
        wa1 = sb("wa1", [P, KB])
        wa2 = sb("wa2", [P, KB, P])
        beta_c = sb("beta_c", [P, 1])
        gate_raw = sb("gate_raw", [P, 5, KB])
        gate_sum = sb("gate_sum", [P, 3, KB])
        gate_bias = sb("gate_bias", [P, 3, KB])
        deg = sb("deg", [P, 1])
        deg_on = sb("deg_on", [P, 1])
        deg_lo = sb("deg_lo", [P, 1])
        deg_p = sb("deg_p", [P, 1])
        dis = sb("dis", [P, 1])
        half = sb("half", [P, GB])
        eps = sb("eps", [P, GB])
        minus = sb("minus", [P, GB])
        adn = sb("adn", [P, P])
        names = ["Z", "R", "V", "U", "UC"]
        hi = {k: sb(f"{k}hi", [P, KB, C], F32R) for k in names}
        lo = {k: sb(f"{k}lo", [P, KB, C], F32R) for k in names}

        X = per_stream("X", [P, GB, C])
        RES = per_stream("RES", [P, GB, C])
        RB = per_stream("RB", [P, GB, C])
        H = per_stream("H", [P, GB, C])
        HT = per_stream("HT", [P, KB, W])
        HTh = per_stream("HTh", [P, KB, W], F32R)
        HTl = per_stream("HTl", [P, KB, W], F32R)
        Ah = per_stream("Ah", [P, KB, W], F32R)
        Al = per_stream("Al", [P, KB, W], F32R)
        QT = per_stream("QT", [P, KB, W])
        QTh = per_stream("QTh", [P, KB, W], F32R)
        QTl = per_stream("QTl", [P, KB, W], F32R)
        TZ = per_stream("TZ", [P, KB, W])
        TR = per_stream("TR", [P, KB, W])
        OUT = per_stream("OUT", [P, GB, C])
        HV = TR
        YT = QT
        HH = TZ
        E1, E2 = TR, QT
        stats = per_stream("stats", [P, GB, 6])
        mv = per_stream("mv", [P, GB, 2])
        ve = per_stream("ve", [P, GB])
        rstd = per_stream("rstd", [P, GB])
        mr = per_stream("mr", [P, GB])
        nmr = per_stream("nmr", [P, GB])
        s1 = per_stream("s1", [P, GB])
        top = per_stream("top", [P, GB])
        tot = per_stream("tot", [P, GB])
        rtot = per_stream("rtot", [P, GB])

        w3r, w4r, w5r = X[1], RES[1], RB[1]
        u3r, u5r, ws = H[1], HT[1], QT[1]

        bank = [[ctx.enter_context(nc.psum_tensor(f"bank{s}{k}", [P, W], F32)) for k in range(4)]
                for s in range(NS)]

        const_in = sem("const_in")
        consts = sem("consts")
        vchain = sem("vchain")
        setup_pe = sem("setup_pe")
        setup_pool = sem("setup_pool")
        setup_pw = sem("setup_pw")
        x_in = signal("x_in", 16)
        stored = signal("stored", 16)
        ln_mv = signal("ln_mv", 3 * 4)
        ln_pool = signal("ln_pool", 4 * 4)
        h_ready = signal("h_ready", 4)
        turned = signal("turned", 2 * (2 + T))
        hT_ready = signal("hT_ready", 2 * 2 + T * 2)
        s_psum = signal("s_psum", 2)
        hh_psum = signal("hh_psum", 2)
        hh_ready = signal("hh_ready", 1)
        soft = signal("soft", 8)
        p_exp = signal("p_exp", 1)
        p_beta = signal("p_beta", 1)
        p_turned = signal("p_turned", 1)
        p_ready = signal("p_ready", 1)
        att_psum = signal("att_psum", 2)
        elu_e = signal("elu_e", 2)
        elu_v = signal("elu_v", 2 * 2)
        res = signal("res", 2 * 3)
        y_psum = signal("y_psum", 4)
        y_ready = signal("y_ready", 4)
        mix_psum = signal("mix_psum", 4)
        rb = signal("rb", 2)
        out_ready = signal("out_ready", 2)
        h_back = signal("h_back", 2 * (T - 1))
        hT_hi = signal("hT_hi", 2 * T)
        hT_lo = signal("hT_lo", 2 * T)
        a_psum = signal("a_psum", 2 * T)
        a_hi = signal("a_hi", 2 * T)
        a_lo = signal("a_lo", 2 * T)
        z_psum = signal("z_psum", 2 * T)
        z_ready = signal("z_ready", 2 * T)
        r_psum = signal("r_psum", 2 * T)
        r_ready = signal("r_ready", 2 * T)
        q_ready = signal("q_ready", 2 * T)
        q_hi = signal("q_hi", 2 * T)
        q_lo = signal("q_lo", 2 * T)
        c_psum = signal("c_psum", 2 * T)
        c_ready = signal("c_ready", 2 * T)
        upd = signal("upd", 2 * 2 * T)

        block = ctx.enter_context(nc.Block())

        loads = [
            (A[:], adj), (AT[:], adjT), (ident[:], ident_in), (beta_c[:], beta), (acol[:], a_cols),
            (W0[:], w0.rearrange("(k p) n -> p k n", p=P)), (W0T[:], w0T.rearrange("(k p) n -> p k n", p=P)),
            (W1[:], w1.rearrange("(k p) n -> p k n", p=P)), (WL[:], wl.rearrange("(k p) n -> p k n", p=P)),
            (B1[:], b1), (BL[:], bl), (gate_raw[:], gate_b),
            (w3r[:], w3T.rearrange("(k p) n -> p k n", p=P)), (w4r[:], w4T.rearrange("(k p) n -> p k n", p=P)),
            (w5r[:], w5T.rearrange("(k p) n -> p k n", p=P)),
            (u3r[:, 0:KB, :], u3T.rearrange("(k p) n -> p k n", p=P)),
            (u5r[:, :, 0:C], u5T.rearrange("(k p) n -> p k n", p=P)),
        ]
        CONSTS = 1

        x_g = x.rearrange("(g b) n c -> g n b c", b=GB)
        out_g = out.rearrange("(g b) n c -> g n b c", b=GB)

        def walk(engine, stage):
            for s, ahead, name in HEAD:
                stage(s, 0, name, False)
            with engine.Fori(0, NG - 1) as g:
                for s, ahead, name in BODY:
                    stage(s, g + ahead if ahead else g, name, False)
            for s, ahead, name in TAIL:
                stage(s, NG - 1, name, True)

        @block.sync
        def _(sp):
            for dst, src in loads:
                sp.dma_start(dst, src).then_inc(const_in, 16)
            for s in range(NS):
                sp.sem_inc(stored.sem[s], 16)
            sp.dma_start(X[0][:], x_g[0]).then_inc(x_in.sem[0], 16)
            sp.wait_ge(consts, CONSTS)
            sp.dma_start(X[1][:], x_g[1]).then_inc(x_in.sem[1], 16)

            def stage(s, g, name, last):
                if name == "u1" and not last:
                    sp.wait_ge(res.sem[s], res.count(g, 2))
                    sp.dma_start(X[s][:], x_g[NS * g + NS + s] if type(g) is int
                                 else x_g[bass.ds(NS * g + NS + s, 1)].rearrange("g n b c -> (g n) b c")
                                 ).then_inc(x_in.sem[s], 16)
                if name == "mix3":
                    sp.wait_ge(out_ready.sem[s], out_ready.count(g, 2))
                    sp.dma_start(out_g[NS * g + s] if type(g) is int
                                 else out_g[bass.ds(NS * g + s, 1)].rearrange("g n b c -> (g n) b c"),
                                 OUT[s][:]).then_inc(stored.sem[s], 16)

            walk(sp, stage)
            for s in range(NS):
                sp.wait_ge(stored.sem[s], stored.count(NG, 16))

        @block.gpsimd
        def _(pool):
            pool.memset(half[:], -0.5).then_inc(setup_pool, 1)
            pool.memset(eps[:], EPS).then_inc(setup_pool, 1)
            pool.memset(minus[:], -1.0).then_inc(setup_pool, 1)
            pool.wait_ge(setup_pool, 3)
            pool.wait_ge(vchain, 3)
            pool.tensor_tensor(deg_p[:], deg_lo[:], half[:, 0:1], ALU.pow).then_inc(setup_pw, 1)

            def layernorm(s, g, layer):
                n = 4 * layer
                pool.wait_ge(ln_mv.sem[s], ln_mv.count(g, 3 * layer + 3))
                pool.tensor_tensor(ve[s][:], mv[s][:, :, 1], eps[:], ALU.add).then_inc(ln_pool.sem[s], 1)
                pool.wait_ge(ln_pool.sem[s], ln_pool.count(g, n + 1))
                pool.tensor_tensor(rstd[s][:], ve[s][:], half[:], ALU.pow).then_inc(ln_pool.sem[s], 1)
                pool.wait_ge(ln_pool.sem[s], ln_pool.count(g, n + 2))
                pool.tensor_tensor(mr[s][:], mv[s][:, :, 0], rstd[s][:], ALU.mult).then_inc(ln_pool.sem[s], 1)
                pool.wait_ge(ln_pool.sem[s], ln_pool.count(g, n + 3))
                pool.tensor_tensor(nmr[s][:], mr[s][:], minus[:], ALU.mult).then_inc(ln_pool.sem[s], 1)

            def add_bias(s, g, layer):
                bias = B1 if layer == 1 else BL
                pool.wait_ge(res.sem[s], res.count(g, 2 if layer == 1 else 6))
                pool.tensor_tensor(RB[s][:], RES[s][:], bias[:].rearrange("p (o c) -> p o c", o=1)
                                   .broadcast_to([P, GB, C]), ALU.add).then_inc(rb.sem[s], 1)

            def stage(s, g, name, last):
                kind, n = split(name)
                if kind == "ln":
                    layernorm(s, g, n)
                if kind == "spread":
                    if n == 1:
                        if type(g) is int and g == 0:
                            pool.wait_ge(consts, CONSTS)
                    add_bias(s, g, n)

            walk(pool, stage)

        @block.scalar
        def _(act):
            def layernorm(s, g, layer):
                src = X[s] if layer == 0 else RES[s]
                if layer == 0 and type(g) is int and g == 0:
                    act.wait_ge(consts, CONSTS)
                act.wait_ge(ln_pool.sem[s], ln_pool.count(g, 4 * layer + 4))
                for b in range(GB):
                    ins = act.activation(H[s][:, b, :], src[:, b, :], ACT.Relu,
                                         bias=nmr[s][:, b:b + 1], scale=rstd[s][:, b:b + 1])
                ins.then_inc(h_ready.sem[s], 1)

            def turned_evac(s, g, first):
                for k in range(KB):
                    act.wait_ge(turned.sem[s], turned.count(g, first + k + 1))
                    act.activation(HT[s][:, k, :], bank[s][k][:], ACT.Copy).then_inc(hT_ready.sem[s], 1)

            def hi_of_h(s, g):
                for k in range(KB):
                    act.wait_ge(hT_ready.sem[s], hT_ready.count(g, 2 + k + 1))
                    act.activation(HTh[s][:, k, :], HT[s][:, k, :], ACT.Copy).then_inc(hT_hi.sem[s], 1)

            def project(s, g):
                for k in range(2):
                    act.wait_ge(hh_psum.sem[s], hh_psum.count(g, k + 1))
                    ins = act.activation(HH[s][:].rearrange("p k (b c) -> p (k b) c", c=C)[:, 2 * k:2 * k + 2, :],
                                         bank[s][2 + k][:].rearrange("p (b c) -> p b c", c=C), ACT.Copy)
                ins.then_inc(hh_ready.sem[s], 1)

            def stage(s, g, name, last):
                kind, n = split(name)
                if kind == "ln":
                    layernorm(s, g, n)
                elif name == "turn0":
                    turned_evac(s, g, 0)
                elif name == "turn2":
                    turned_evac(s, g, 2)
                    hi_of_h(s, g)
                elif kind == "project":
                    project(s, g)
                elif kind == "softmax":
                    act.wait_ge(soft.sem[s], soft.count(g, 6))
                    act.activation(E1[s][:, 0, :], E2[s][:, 0, :], ACT.Exp).then_inc(p_exp.sem[s], 1)
                elif kind == "turn_p":
                    act.wait_ge(p_turned.sem[s], p_turned.count(g, 1))
                    act.activation(E2[s][:, 1, :], bank[s][0][:], ACT.Copy).then_inc(p_ready.sem[s], 1)
                elif kind == "attend":
                    for k in range(2):
                        act.wait_ge(att_psum.sem[s], att_psum.count(g, k + 1))
                        act.activation(E1[s][:, k, :], bank[s][2 + k][:], ACT.Exp).then_inc(elu_e.sem[s], 1)
                elif kind == "spread":
                    f = 0 if n == 1 else 2
                    for k in range(2):
                        act.wait_ge(y_psum.sem[s], y_psum.count(g, f + k + 1))
                        act.activation(YT[s][:, k, :], bank[s][k][:], ACT.Copy).then_inc(y_ready.sem[s], 1)
                elif kind == "back" and n < T:
                    for k in range(2):
                        act.wait_ge(turned.sem[s], turned.count(g, 4 + 2 * (n - 1) + k + 1))
                        act.activation(H[s][:, 2 * k:2 * k + 2, :],
                                       bank[s][2 + k][:].rearrange("p (b c) -> p b c", c=C),
                                       ACT.Copy).then_inc(h_back.sem[s], 1)
                elif kind == "a":
                    for k in range(KB):
                        act.wait_ge(a_psum.sem[s], a_psum.count(g, 2 * n + k + 1))
                        act.activation(Ah[s][:, k, :], bank[s][2 + k][:], ACT.Copy).then_inc(a_hi.sem[s], 1)
                elif kind == "z":
                    for k in range(KB):
                        act.wait_ge(z_psum.sem[s], z_psum.count(g, 2 * n + k + 1))
                        act.activation(TZ[s][:, k, :], bank[s][k][:], ACT.Tanh, scale=0.5,
                                       bias=gate_bias[:, 0, k:k + 1]).then_inc(z_ready.sem[s], 1)
                elif kind == "r":
                    for k in range(KB):
                        act.wait_ge(r_psum.sem[s], r_psum.count(g, 2 * n + k + 1))
                        act.activation(TR[s][:, k, :], bank[s][k][:], ACT.Tanh, scale=0.5,
                                       bias=gate_bias[:, 1, k:k + 1]).then_inc(r_ready.sem[s], 1)
                    for k in range(KB):
                        act.wait_ge(q_ready.sem[s], q_ready.count(g, 2 * n + k + 1))
                        act.activation(QTh[s][:, k, :], QT[s][:, k, :], ACT.Copy).then_inc(q_hi.sem[s], 1)
                elif kind == "c":
                    for k in range(KB):
                        act.wait_ge(c_psum.sem[s], c_psum.count(g, 2 * n + k + 1))
                        act.activation(HV[s][:, k, :], bank[s][2 + k][:], ACT.Tanh,
                                       bias=gate_bias[:, 2, k:k + 1]).then_inc(c_ready.sem[s], 1)
                    if n < T - 1:
                        for k in range(KB):
                            act.wait_ge(hT_ready.sem[s], hT_ready.count(g, 4 + 2 * n + k + 1))
                            act.activation(HTh[s][:, k, :], HT[s][:, k, :], ACT.Copy).then_inc(hT_hi.sem[s], 1)

            walk(act, stage)

        @block.vector
        def _(dve):
            dve.wait_ge(const_in, 16 * len(loads))
            chain = [0]

            def link(ins):
                chain[0] += 1
                ins.then_inc(vchain, 1)
                dve.wait_ge(vchain, chain[0])

            link(dve.tensor_reduce(deg[:], A[:], AX.X, ALU.add))
            link(dve.tensor_scalar(deg_on[:], deg[:], 0.0, None, ALU.is_gt))
            link(dve.tensor_scalar(deg_lo[:], deg[:], TINY, None, ALU.max))
            dve.wait_ge(setup_pw, 1)
            link(dve.tensor_tensor(dis[:], deg_p[:], deg_on[:], ALU.mult))
            link(dve.tensor_scalar(adn[:], A[:], dis[:], None, ALU.mult))
            link(dve.tensor_copy(a2bc[:], acol[:, KB:2 * KB].rearrange("p (k o) -> p k o", o=1)
                                 .broadcast_to([P, KB, P])))
            link(dve.tensor_scalar(betaI[:], ident[:], beta_c[:], None, ALU.mult))
            link(dve.tensor_tensor(gate_sum[:, 0:2, :], gate_raw[:, 0:2, :],
                                   gate_raw[:, 3:4, :].broadcast_to([P, 2, KB]), ALU.add))
            link(dve.tensor_tensor(gate_sum[:, 2, :], gate_raw[:, 2, :], gate_raw[:, 4, :], ALU.add))
            link(dve.tensor_scalar(gate_bias[:, 0:2, :], gate_sum[:, 0:2, :], 0.5, None, ALU.mult))
            link(dve.tensor_copy(gate_bias[:, 2, :], gate_sum[:, 2, :]))
            w = ws[:, :, 0:C]
            w3s, w4s = w3r[:, 0:KB, :], w4r[:, 0:KB, :]

            def halves(k, src):
                link(dve.tensor_copy(hi[k][:], src))
                link(dve.tensor_tensor(lo[k][:], src, hi[k][:].bitcast(F32), ALU.subtract))

            link(dve.tensor_tensor(w3s, w3r[:, 0:KB, :], w3r[:, KB:2 * KB, :], ALU.add))
            halves("Z", w3s)
            link(dve.tensor_tensor(w4s, w4r[:, 0:KB, :], w4r[:, KB:2 * KB, :], ALU.add))
            link(dve.tensor_tensor(w, w4s, w3s, ALU.subtract))
            halves("R", w)
            link(dve.tensor_tensor(w5r[:, 0:KB, :], w5r[:, 0:KB, :], w5r[:, KB:2 * KB, :], ALU.add))
            halves("V", w5r[:, 0:KB, :])
            halves("U", u3r[:, 0:KB, :])
            link(dve.tensor_scalar(w, u5r[:, :, 0:C], 0.5, None, ALU.mult))
            halves("UC", w)
            dve.wait_ge(setup_pe, 1)
            link(dve.tensor_scalar(NT[:], bank[0][0][:, 0:P], dis[:], None, ALU.mult))
            link(dve.tensor_copy(wa1[:], bank[0][1][:, 0:KB]))
            link(dve.tensor_copy(wa2[:], bank[0][2][:, 0:KB * P].rearrange("p (k m) -> p k m", m=P)))
            dve.engine_nop().then_inc(consts, 1)

            def layernorm(s, g, layer):
                src = X[s] if layer == 0 else RES[s]
                if layer == 0:
                    dve.wait_ge(x_in.sem[s], x_in.count(g, 16))
                else:
                    dve.wait_ge(res.sem[s], res.count(g, 2 * layer))
                for b in range(GB):
                    ins = dve.bn_stats(stats[s][:, b, :], src[:, b, :])
                ins.then_inc(ln_mv.sem[s], 1)
                dve.wait_ge(ln_mv.sem[s], ln_mv.count(g, 3 * layer + 1))
                dve.sem_inc(ln_mv.sem[s], 1)
                for b in range(GB):
                    ins = dve.bn_aggr(mv[s][:, b, :], stats[s][:, b, :])
                ins.then_inc(ln_mv.sem[s], 1)

            def softmax(s, g):
                def by_graph(ap):
                    return ap.rearrange("p (b m) -> p b m", m=P)

                def wide(col):
                    return col[:].rearrange("p (b o) -> p b o", o=1).broadcast_to([P, GB, P])

                def step(ins, n):
                    ins.then_inc(soft.sem[s], 1)
                    dve.wait_ge(soft.sem[s], soft.count(g, n))

                dve.wait_ge(s_psum.sem[s], s_psum.count(g, 2))
                e1, e2 = by_graph(E1[s][:, 0, :]), by_graph(E2[s][:, 0, :])
                step(dve.tensor_copy(s1[s][:], bank[s][1][:, 0:GB]), 1)
                step(dve.tensor_tensor(e1, by_graph(bank[s][0][:]), wide(s1[s]), ALU.add), 2)
                step(dve.scalar_tensor_tensor(e2, e1, SLOPE, e1, ALU.mult, ALU.max), 3)
                step(dve.tensor_tensor(e1, e2, A[:].rearrange("p (o m) -> p o m", o=1)
                                       .broadcast_to([P, GB, P]), ALU.mult), 4)
                step(dve.tensor_reduce(top[s][:], e1, AX.X, ALU.max), 5)
                dve.tensor_tensor(e2, e1, wide(top[s]), ALU.subtract).then_inc(soft.sem[s], 1)
                dve.wait_ge(p_exp.sem[s], p_exp.count(g, 1))
                step(dve.tensor_reduce(tot[s][:], e1, AX.X, ALU.add), 7)
                step(dve.reciprocal(rtot[s][:], tot[s][:]), 8)
                for b in range(GB):
                    ins = dve.scalar_tensor_tensor(E2[s][:, 0, b * P:(b + 1) * P], E1[s][:, 0, b * P:(b + 1) * P],
                                                   rtot[s][:, b:b + 1], betaI[:], ALU.mult, ALU.add)
                ins.then_inc(p_beta.sem[s], 1)

            def attend(s, g):
                for k in range(2):
                    dve.wait_ge(elu_e.sem[s], elu_e.count(g, k + 1))
                    dve.tensor_scalar(E2[s][:, k, :], E1[s][:, k, :], 1.0, -1.0, ALU.min, ALU.add)\
                       .then_inc(elu_v.sem[s], 1)
                    dve.wait_ge(elu_v.sem[s], elu_v.count(g, 2 * k + 1))
                    dve.tensor_tensor(E1[s][:, k, :], bank[s][2 + k][:], E2[s][:, k, :], ALU.max)\
                       .then_inc(elu_v.sem[s], 1)
                    dve.wait_ge(elu_v.sem[s], elu_v.count(g, 2 * k + 2))
                    dve.tensor_tensor(RES[s][:, 2 * k:2 * k + 2, :],
                                      E1[s][:, k, :].rearrange("p (b c) -> p b c", c=C),
                                      X[s][:, 2 * k:2 * k + 2, :], ALU.add).then_inc(res.sem[s], 1)

            def stage(s, g, name, last):
                kind, n = split(name)
                if kind == "ln":
                    layernorm(s, g, n)
                elif kind == "softmax":
                    softmax(s, g)
                elif kind == "attend":
                    attend(s, g)
                elif name == "mix1":
                    dve.wait_ge(rb.sem[s], rb.count(g, 1))
                    for k in range(2):
                        dve.wait_ge(mix_psum.sem[s], mix_psum.count(g, k + 1))
                        dve.tensor_tensor(RES[s][:, 2 * k:2 * k + 2, :],
                                          bank[s][2 + k][:].rearrange("p (b c) -> p b c", c=C),
                                          RB[s][:, 2 * k:2 * k + 2, :], ALU.add).then_inc(res.sem[s], 1)
                elif name == "mix3":
                    dve.wait_ge(rb.sem[s], rb.count(g, 2))
                    dve.wait_ge(stored.sem[s], stored.count(g, 16))
                    for k in range(2):
                        dve.wait_ge(mix_psum.sem[s], mix_psum.count(g, 2 + k + 1))
                        dve.tensor_tensor(OUT[s][:, 2 * k:2 * k + 2, :],
                                          bank[s][2 + k][:].rearrange("p (b c) -> p b c", c=C),
                                          RB[s][:, 2 * k:2 * k + 2, :], ALU.add).then_inc(out_ready.sem[s], 1)
                elif name == "turn2":
                    for k in range(KB):
                        dve.wait_ge(hT_hi.sem[s], hT_hi.count(g, k + 1))
                        dve.tensor_tensor(HTl[s][:, k, :], HT[s][:, k, :], HTh[s][:, k, :].bitcast(F32),
                                          ALU.subtract).then_inc(hT_lo.sem[s], 1)
                elif kind == "a":
                    for k in range(KB):
                        dve.wait_ge(a_hi.sem[s], a_hi.count(g, 2 * n + k + 1))
                        dve.tensor_tensor(Al[s][:, k, :], bank[s][2 + k][:], Ah[s][:, k, :].bitcast(F32),
                                          ALU.subtract).then_inc(a_lo.sem[s], 1)
                elif kind == "r":
                    for k in range(KB):
                        dve.wait_ge(r_ready.sem[s], r_ready.count(g, 2 * n + k + 1))
                        dve.scalar_tensor_tensor(QT[s][:, k, :], TR[s][:, k, :], 1.0, HT[s][:, k, :],
                                                 ALU.add, ALU.mult).then_inc(q_ready.sem[s], 1)
                    for k in range(KB):
                        dve.wait_ge(q_hi.sem[s], q_hi.count(g, 2 * n + k + 1))
                        dve.tensor_tensor(QTl[s][:, k, :], QT[s][:, k, :], QTh[s][:, k, :].bitcast(F32),
                                          ALU.subtract).then_inc(q_lo.sem[s], 1)
                elif kind == "c":
                    for k in range(KB):
                        m = 2 * (2 * n + k)
                        dve.wait_ge(c_ready.sem[s], c_ready.count(g, 2 * n + k + 1))
                        dve.tensor_tensor(QT[s][:, k, :], HV[s][:, k, :], HT[s][:, k, :], ALU.subtract)\
                           .then_inc(upd.sem[s], 1)
                        dve.wait_ge(upd.sem[s], upd.count(g, m + 1))
                        dve.scalar_tensor_tensor(HV[s][:, k, :], TZ[s][:, k, :], 1.0, QT[s][:, k, :],
                                                 ALU.add, ALU.mult).then_inc(upd.sem[s], 1)
                        dve.wait_ge(upd.sem[s], upd.count(g, m + 2))
                        dve.scalar_tensor_tensor(HT[s][:, k, :], HV[s][:, k, :], 0.5, HT[s][:, k, :],
                                                 ALU.mult, ALU.add).then_inc(hT_ready.sem[s], 1)
                    if n < T - 1:
                        for k in range(KB):
                            dve.wait_ge(hT_hi.sem[s], hT_hi.count(g, 2 * (n + 1) + k + 1))
                            dve.tensor_tensor(HTl[s][:, k, :], HT[s][:, k, :], HTh[s][:, k, :].bitcast(F32),
                                              ALU.subtract).then_inc(hT_lo.sem[s], 1)
                elif kind == "back" and n == T:
                    for k in range(2):
                        dve.wait_ge(turned.sem[s], turned.count(g, 4 + 2 * (n - 1) + k + 1))
                        dve.tensor_tensor(RES[s][:, 2 * k:2 * k + 2, :],
                                          bank[s][2 + k][:].rearrange("p (b c) -> p b c", c=C),
                                          RES[s][:, 2 * k:2 * k + 2, :], ALU.add).then_inc(res.sem[s], 1)

            walk(dve, stage)

        @block.tensor
        def _(pe):
            pe.wait_ge(const_in, 16 * len(loads))
            pe.wait_ge(vchain, 6)
            pe.transpose(bank[0][0][:, 0:P], adn[:], ident[:])
            for c in range(KB):
                for k in range(KB):
                    pe.matmul(bank[0][1][:, c:c + 1], W0T[:, k, c * P:(c + 1) * P], acol[:, k:k + 1],
                              start=(k == 0), stop=(k == KB - 1))
            for c in range(KB):
                for k in range(KB):
                    ins = pe.matmul(bank[0][2][:, c * P:(c + 1) * P], W0T[:, k, c * P:(c + 1) * P],
                                    a2bc[:, k, :], start=(k == 0), stop=(k == KB - 1))
            ins.then_inc(setup_pe, 1)
            pe.wait_ge(consts, CONSTS)

            def turn(s, g, first):
                for k in range(KB):
                    for b in range(GB):
                        ins = pe.transpose(bank[s][k][:, b * P:(b + 1) * P], H[s][:, b, k * P:(k + 1) * P], ident[:])
                    ins.then_inc(turned.sem[s], 1)

            def back(s, g):
                for b in range(GB):
                    for k in range(KB):
                        at = (b % 2) * C + k * P
                        ins = pe.transpose(bank[s][2 + b // 2][:, at:at + P], HT[s][:, k, b * P:(b + 1) * P], ident[:])
                    if b % 2:
                        ins.then_inc(turned.sem[s], 1)

            def spread(s, g, first, right, done):
                for k in range(KB):
                    for b in range(GB):
                        ins = pe.matmul(bank[s][first + k][:, b * P:(b + 1) * P], H[s][:, b, k * P:(k + 1) * P],
                                        right[:], start=True, stop=True)
                    ins.then_inc(done.sem[s], 1)

            def rows(s, g, left, right, done):
                for b in range(GB):
                    for k in range(KB):
                        ins = pe.matmul(bank[s][2 + b // 2][:, (b % 2) * C:(b % 2 + 1) * C],
                                        left[s][:, k, b * P:(b + 1) * P], right[:, k, :],
                                        start=(k == 0), stop=(k == KB - 1))
                    if b % 2:
                        ins.then_inc(done.sem[s], 1)

            def gate(s, g, key, mh, ml, first, start, stop, done, at, lo_ready):
                for o in range(KB):
                    n = 0
                    for wk, m in ((hi, mh), (lo, mh), (hi, ml)):
                        for k in range(KB):
                            if o == 0 and m is ml:
                                pe.wait_ge(lo_ready.sem[s], lo_ready.count(g, at + k + 1))
                            ins = pe.matmul(bank[s][first + o][:], wk[key][:, k, o * P:(o + 1) * P], m[s][:, k, :],
                                            start=(start and n == 0), stop=(stop and n == 3 * KB - 1),
                                            skip_group_check=True)
                            n += 1
                    if done is not None:
                        ins.then_inc(done.sem[s], 1)

            def stage(s, g, name, last):
                kind, n = split(name)
                if name == "turn0":
                    pe.wait_ge(h_ready.sem[s], h_ready.count(g, 1))
                    turn(s, g, 0)
                elif kind == "scores":
                    pe.wait_ge(hT_ready.sem[s], hT_ready.count(g, 2))
                    for k in range(KB):
                        ins = pe.matmul(bank[s][0][:], wa2[:, k, :], HT[s][:, k, :], start=(k == 0), stop=(k == KB - 1))
                    ins.then_inc(s_psum.sem[s], 1)
                    for b in range(GB):
                        for k in range(KB):
                            ins = pe.matmul(bank[s][1][:, b:b + 1], HT[s][:, k, b * P:(b + 1) * P], wa1[:, k:k + 1],
                                            start=(k == 0), stop=(k == KB - 1))
                    ins.then_inc(s_psum.sem[s], 1)
                elif kind == "project":
                    rows(s, g, HT, W0, hh_psum)
                elif kind == "turn_p":
                    pe.wait_ge(p_beta.sem[s], p_beta.count(g, 1))
                    for b in range(GB):
                        ins = pe.transpose(bank[s][0][:, b * P:(b + 1) * P], E2[s][:, 0, b * P:(b + 1) * P], ident[:])
                    ins.then_inc(p_turned.sem[s], 1)
                elif kind == "attend":
                    pe.wait_ge(hh_ready.sem[s], hh_ready.count(g, 1))
                    pe.wait_ge(p_ready.sem[s], p_ready.count(g, 1))
                    hh = HH[s][:].rearrange("p k (b c) -> p (k b) c", c=C)
                    for b in range(GB):
                        ins = pe.matmul(bank[s][2 + b // 2][:, (b % 2) * C:(b % 2 + 1) * C],
                                        E2[s][:, 1, b * P:(b + 1) * P], hh[:, b, :], start=True, stop=True)
                        if b % 2:
                            ins.then_inc(att_psum.sem[s], 1)
                elif kind == "spread":
                    pe.wait_ge(h_ready.sem[s], h_ready.count(g, 2 if n == 1 else 4))
                    spread(s, g, 0, NT if n == 1 else AT, y_psum)
                elif kind == "mix":
                    pe.wait_ge(y_ready.sem[s], y_ready.count(g, 2 if n == 1 else 4))
                    rows(s, g, YT, W1 if n == 1 else WL, mix_psum)
                elif name == "turn2":
                    pe.wait_ge(h_ready.sem[s], h_ready.count(g, 3))
                    turn(s, g, 2)
                elif kind == "back":
                    pe.wait_ge(hT_ready.sem[s], hT_ready.count(g, 4 + 2 * n))
                    back(s, g)
                elif kind == "u":
                    pe.wait_ge(hT_hi.sem[s], hT_hi.count(g, 2 * n + 2))
                    gate(s, g, "U", HTh, HTl, 0, True, False, None, 2 * n, hT_lo)
                elif kind == "a":
                    if n:
                        pe.wait_ge(h_back.sem[s], h_back.count(g, 2 * n))
                    spread(s, g, 2, AT, a_psum)
                elif kind == "z":
                    pe.wait_ge(a_hi.sem[s], a_hi.count(g, 2 * n + 2))
                    gate(s, g, "Z", Ah, Al, 0, False, True, z_psum, 2 * n, a_lo)
                elif kind == "v":
                    gate(s, g, "V", Ah, Al, 2, True, False, None, 2 * n, a_lo)
                elif kind == "r":
                    pe.wait_ge(z_ready.sem[s], z_ready.count(g, 2 * n + 2))
                    gate(s, g, "R", Ah, Al, 0, False, True, r_psum, 2 * n, a_lo)
                elif kind == "c":
                    pe.wait_ge(q_hi.sem[s], q_hi.count(g, 2 * n + 2))
                    gate(s, g, "UC", QTh, QTl, 2, False, True, c_psum, 2 * n, q_lo)

            walk(pe, stage)


def kernel(x, adj, L0_gnn_W, L0_gnn_a, L0_gnn_beta, L1_gnn_weight, L1_gnn_bias, L2_gnn_w3_w, L2_gnn_w3_b,
           L2_gnn_u3_w, L2_gnn_u3_b, L2_gnn_w4_w, L2_gnn_w4_b, L2_gnn_w5_w, L2_gnn_w5_b, L2_gnn_u5_w,
           L2_gnn_u5_b, L3_gnn_weight, L3_gnn_bias):
    import numpy as np
    import concourse.bacc as bacc
    from concourse.bass_utils import run_bass_kernel_spmd

    def rows(v):
        return np.broadcast_to(np.asarray(v)[None, :], (P, C))

    def blocks(v):
        return np.asarray(v).reshape(KB, P).T

    host = {
        "x": x,
        "adj": adj,
        "adjT": np.asarray(adj).T,
        "ident": np.eye(P, dtype=np.float32),
        "w0": L0_gnn_W,
        "w0T": np.asarray(L0_gnn_W).T,
        "a_cols": np.asarray(L0_gnn_a).reshape(2 * KB, P).T,
        "beta": np.broadcast_to(np.asarray(L0_gnn_beta)[None, :], (P, 1)),
        "w1": L1_gnn_weight,
        "b1": rows(L1_gnn_bias),
        "w3T": np.asarray(L2_gnn_w3_w).T,
        "w4T": np.asarray(L2_gnn_w4_w).T,
        "w5T": np.asarray(L2_gnn_w5_w).T,
        "u3T": np.asarray(L2_gnn_u3_w).T,
        "u5T": np.asarray(L2_gnn_u5_w).T,
        "gate_b": np.stack([blocks(v) for v in (L2_gnn_w3_b, L2_gnn_w4_b, L2_gnn_w5_b, L2_gnn_u3_b, L2_gnn_u5_b)], axis=1),
        "wl": L3_gnn_weight,
        "bl": rows(L3_gnn_bias),
    }
    host = {k: np.ascontiguousarray(v) for k, v in host.items()}
    nc = bacc.Bacc("TRN2", target_bir_lowering=False, num_devices=1)
    args = [nc.dram_tensor(k + "_dram", v.shape, mybir.dt.from_np(v.dtype), kind="ExternalInput").ap() for k, v in host.items()]
    args.append(nc.dram_tensor("out_dram", (B, P, C), F32, kind="ExternalOutput").ap())
    build(nc, *args)
    r = run_bass_kernel_spmd(nc, [{k + "_dram": v for k, v in host.items()}], core_ids=[0])
    return r.results[0]["out_dram"]
```

```python
import concourse.bass as bass
from concourse import mybir
from contextlib import ExitStack

F32 = mybir.dt.float32
F32R = mybir.dt.float32r
ALU = mybir.AluOpType
ACT = mybir.ActivationFunctionType
AX = mybir.AxisListType

P = 128
C = 256
KB = C // P
B = 64
GB = 2
NS = 4
NG = B // GB // NS
W = GB * P
T = 3
EPS = 1e-5
SLOPE = 0.2
TINY = 1.1754943508222875e-38

PE_ORDER = """
    v2:3 r2:3 turn0:0 mix1:1 project:0 back1:2 scores:0 u1:2 a1:2 c2:3 z1:2 turn2:1 v1:2 r1:2
    back3:3 turn_p:0 u0:1 attend:0 a0:1 c1:2 z0:1 v0:1 r0:1 back2:2 spread3:3 u2:2 a2:2 mix3:3 c0:1
    z2:2 spread1:0
"""
ACT_ORDER = """
    tc0:2 tz2:3 y1_hi:1 norm0:0 h_hi1:2 tr2:3 h0_hi:0 q_hi2:3 hh:0 natural1:2 a_hi1:2 norm2:1 tc2:3
    exp_p:0 tz1:2 hT:1 tr1:2 p_hi:0 q_hi1:2 a_hi0:1 exp_v:0 tc1:2 tz0:1 norm3:3 h_hi2:2 tr0:1
    natural2:2 y3_hi:3 q_hi0:1 a_hi2:2 norm1:0
"""
DVE_ORDER = """
    a_lo2:3 stats0:0 aggr0:0 upd0:2 y1_lo:1 h_lo1:2 q2:3 h0_lo:0 x2:1 stats2:1 q_lo2:3 aggr2:1 s1:0
    hh_lo:0 soft_a:0 a_lo1:2 upd2:3 soft_b:0 h_lo0:1 q1:2 p_lo:0 x3:3 q_lo1:2 stats3:3 aggr3:3
    a_lo0:1 upd1:2 elu:0 q0:1 h_lo2:2 stats1:0 q_lo0:1 aggr1:0 y3_lo:3 out:3
"""
POOL_ORDER = """
    ln0:0 bias1:1 ln2:1 ln3:3 bias3:3 ln1:0
"""


SP_ORDER = f"load:{NS - 1} store:{NS - 1}"


def parts(order):
    return [(p.split(":")[0], int(p.split(":")[1])) for p in order.split()]


def kind_of(part):
    kind = part.rstrip("0123456789")
    return kind, int("0" + part[len(kind):])


def walk(engine, order, do):
    lead = NS - 1
    for q in range(lead):
        for part, ago in parts(order):
            if q >= ago:
                do(part, (q - ago) % NS, (q - ago) // NS)
    with engine.Fori(0, NG - 1) as i:
        for q in range(lead, lead + NS):
            for part, ago in parts(order):
                later = (q - ago) // NS
                do(part, (q - ago) % NS, i + later if later else i)
    for q in range(NS * NG - 1, NS * NG + lead):
        for part, ago in parts(order):
            if q - ago < NS * NG:
                do(part, (q - ago) % NS, (q - ago) // NS)


class Signal:

    def __init__(self, ctx, nc, name, events):
        self.sem = [ctx.enter_context(nc.semaphore(f"{name}_{s}")) for s in range(NS)]
        self.events = None if type(events) is int else events
        self.per_group = events if type(events) is int else len(events)

    def count(self, g, n):
        return g * self.per_group + (n if self.events is None else self.events.index(n) + 1)


def build(nc, x, adj, adjT, ident_in, w0, w0T, a_cols, a1_rows, beta, w1, b1, w3T, w4T, w5T, u3T, u5T, gate_b, wl, bl, out):
    with ExitStack() as ctx:
        def sb(name, shape, dt=F32):
            return ctx.enter_context(nc.sbuf_tensor(name, shape, dt))

        def sem(name):
            return ctx.enter_context(nc.semaphore(name))

        def signal(name, per_group):
            return Signal(ctx, nc, name, per_group)

        def per_stream(name, shape, dt=F32):
            return [sb(f"{name}_{s}", shape, dt) for s in range(NS)]

        A = sb("A", [P, P])
        AT = sb("AT", [P, P])
        NT = sb("NT", [P, P])
        ident = sb("ident", [P, P])
        betaI = sb("betaI", [P, P])
        W0T = sb("W0T", [P, KB, C])
        B1 = sb("B1", [P, C])
        BL = sb("BL", [P, C])
        acol = sb("acol", [P, 2 * KB])
        a2bc = sb("a2bc", [P, KB, P])
        beta_c = sb("beta_c", [P, 1])
        gate_raw = sb("gate_raw", [P, 5, KB])
        gate_sum = sb("gate_sum", [P, 3, KB])
        gate_bias = sb("gate_bias", [P, 3, KB])
        deg = sb("deg", [P, 1])
        deg_on = sb("deg_on", [P, 1])
        deg_lo = sb("deg_lo", [P, 1])
        deg_p = sb("deg_p", [P, 1])
        dis = sb("dis", [P, 1])
        a1bc = sb("a1bc", [P, C])
        half = sb("half", [P, GB])
        eps = sb("eps", [P, GB])
        minus = sb("minus", [P, GB])
        adn = sb("adn", [P, P])
        names = {"Z": C, "R": C, "V": C, "U": C, "UC": C, "W0": C, "W1": C, "WL": C, "WA2": P}
        hi = {k: sb(f"{k}hi", [P, KB, n], F32R) for k, n in names.items()}
        lo = {k: sb(f"{k}lo", [P, KB, n], F32R) for k, n in names.items()}

        X = per_stream("X", [P, GB, C])
        RES = per_stream("RES", [P, GB, C])
        RB = per_stream("RB", [P, GB, C])
        OUT = per_stream("OUT", [P, GB, C])
        H = per_stream("H", [P, GB, C])
        HT = per_stream("HT", [P, KB, W])
        HTh = per_stream("HTh", [P, KB, W], F32R)
        HTl = per_stream("HTl", [P, KB, W], F32R)
        Ah = per_stream("Ah", [P, KB, W], F32R)
        Al = per_stream("Al", [P, KB, W], F32R)
        QT = per_stream("QT", [P, KB, W])
        QTh = per_stream("QTh", [P, KB, W], F32R)
        QTl = per_stream("QTl", [P, KB, W], F32R)
        TZ = per_stream("TZ", [P, KB, W])
        TR = per_stream("TR", [P, KB, W])
        HV = TR
        HH, HHh, HHl = TZ, Ah, Al
        PTh, PTl = QTh, QTl
        E1, E2 = TR, QT
        stats = per_stream("stats", [P, GB, 6])
        mv = per_stream("mv", [P, GB, 2])
        ve = per_stream("ve", [P, GB])
        rstd = per_stream("rstd", [P, GB])
        mr = per_stream("mr", [P, GB])
        nmr = per_stream("nmr", [P, GB])
        s1 = per_stream("s1", [P, GB])
        top = per_stream("top", [P, GB])
        tot = per_stream("tot", [P, GB])
        rtot = per_stream("rtot", [P, GB])

        w3r = [X[1], RES[1]]
        w4r = [RB[1], H[1]]
        w5r = [X[2], RES[2]]
        u3r, u5r = RB[2], H[2]
        w0r, w1r, wlr = X[3], RES[3], RB[3]
        w3s, w4s, ws = HT[1], QT[1], HT[2]

        bank = [[ctx.enter_context(nc.psum_tensor(f"bank{s}{k}", [P, KB, W], F32)) for k in range(2)]
                for s in range(NS)]

        const_in = sem("const_in")
        consts = sem("consts")
        vchain = sem("vchain")
        setup_pe = sem("setup_pe")
        setup_pool = sem("setup_pool")
        setup_pw = sem("setup_pw")
        x_in = signal("x_in", 16)
        stored = signal("stored", 16)
        ln_mv = signal("ln_mv", 3 * 4)
        ln_pool = signal("ln_pool", 4 * 4)
        h_ready = signal("h_ready", 4)
        in_bank0 = signal("in_bank0", ["turn0", "scores", "turn_p", "spread1", "turn2"]
                          + [f"{k}{t}" for t in range(T) for k in "zr"] + ["spread3"])
        in_bank1 = signal("in_bank1", ["project", "attend", "mix1"]
                          + [k for t in range(T) for k in (f"a{t}", f"c{t}", f"back{t + 1}")] + ["mix3"])
        hT_ready = signal("hT_ready", 1 + T)
        hh_ready = signal("hh_ready", 1)
        soft = signal("soft", 8)
        p_exp = signal("p_exp", 1)
        p_beta = signal("p_beta", 1)
        elu_e = signal("elu_e", 1)
        elu_v = signal("elu_v", 2)
        res = signal("res", 3)
        rb = signal("rb", 2)
        out_ready = signal("out_ready", 1)
        h_back = signal("h_back", T - 1)
        hT_hi = signal("hT_hi", 1 + T)
        hT_lo = signal("hT_lo", 1 + T)
        a_hi = signal("a_hi", ["project", "spread1"] + [f"a{t}" for t in range(T)] + ["spread3"])
        a_lo = signal("a_lo", a_hi.events)
        z_ready = signal("z_ready", T)
        r_ready = signal("r_ready", T)
        q_ready = signal("q_ready", T)
        q_hi = signal("q_hi", ["turn_p"] + [f"r{t}" for t in range(T)])
        q_lo = signal("q_lo", q_hi.events)
        c_ready = signal("c_ready", T)
        upd = signal("upd", 2 * T)

        block = ctx.enter_context(nc.Block())

        def by_block(w):
            return w.rearrange("(k p) n -> p k n", p=P)

        loads = [
            (A[:], adj), (AT[:], adjT), (ident[:], ident_in), (beta_c[:], beta), (acol[:], a_cols),
            (a1bc[:], a1_rows), (W0T[:], by_block(w0T)), (B1[:], b1), (BL[:], bl), (gate_raw[:], gate_b),
            (w3r[0][:], by_block(w3T[0:C, :])), (w3r[1][:], by_block(w3T[C:2 * C, :])),
            (w4r[0][:], by_block(w4T[0:C, :])), (w4r[1][:], by_block(w4T[C:2 * C, :])),
            (w5r[0][:], by_block(w5T[0:C, :])), (w5r[1][:], by_block(w5T[C:2 * C, :])),
            (u3r[:], by_block(u3T)), (u5r[:], by_block(u5T)),
            (w0r[:], by_block(w0)), (w1r[:], by_block(w1)), (wlr[:], by_block(wl)),
        ]

        x_g = x.rearrange("(g b) n c -> g n b c", b=GB)
        out_g = out.rearrange("(g b) n c -> g n b c", b=GB)

        def group(dram, i):
            return dram[i] if type(i) is int else dram[bass.ds(i, 1)].rearrange("g n b c -> (g n) b c")

        @block.sync
        def _(sp):
            for dst, src in loads:
                sp.dma_start(dst, src).then_inc(const_in, 16)
            for s in range(NS):
                sp.sem_inc(stored.sem[s], 16)
            sp.dma_start(X[0][:], x_g[0]).then_inc(x_in.sem[0], 16)
            sp.wait_ge(consts, 1)
            for s in range(1, NS):
                sp.dma_start(X[s][:], x_g[s]).then_inc(x_in.sem[s], 16)

            def do(part, s, g):
                if part == "load" and not (type(g) is int and g == NG - 1):
                    sp.wait_ge(res.sem[s], res.count(g, 1))
                    sp.dma_start(X[s][:], group(x_g, NS * g + NS + s)).then_inc(x_in.sem[s], 16)
                if part == "store":
                    sp.wait_ge(out_ready.sem[s], out_ready.count(g, 1))
                    sp.dma_start(group(out_g, NS * g + s), OUT[s][:]).then_inc(stored.sem[s], 16)

            walk(sp, SP_ORDER, do)
            for s in range(NS):
                sp.wait_ge(stored.sem[s], stored.count(NG, 16))

        @block.gpsimd
        def _(pool):
            pool.memset(half[:], -0.5).then_inc(setup_pool, 1)
            pool.memset(eps[:], EPS).then_inc(setup_pool, 1)
            pool.memset(minus[:], -1.0).then_inc(setup_pool, 1)
            pool.wait_ge(setup_pool, 3)
            pool.wait_ge(vchain, 3)
            pool.tensor_tensor(deg_p[:], deg_lo[:], half[:, 0:1], ALU.pow).then_inc(setup_pw, 1)
            pool.wait_ge(consts, 1)

            def layernorm(s, g, layer):
                n = 4 * layer
                pool.wait_ge(ln_mv.sem[s], ln_mv.count(g, 3 * layer + 3))
                pool.tensor_tensor(ve[s][:], mv[s][:, :, 1], eps[:], ALU.add).then_inc(ln_pool.sem[s], 1)
                pool.wait_ge(ln_pool.sem[s], ln_pool.count(g, n + 1))
                pool.tensor_tensor(rstd[s][:], ve[s][:], half[:], ALU.pow).then_inc(ln_pool.sem[s], 1)
                pool.wait_ge(ln_pool.sem[s], ln_pool.count(g, n + 2))
                pool.tensor_tensor(mr[s][:], mv[s][:, :, 0], rstd[s][:], ALU.mult).then_inc(ln_pool.sem[s], 1)
                pool.wait_ge(ln_pool.sem[s], ln_pool.count(g, n + 3))
                pool.tensor_tensor(nmr[s][:], mr[s][:], minus[:], ALU.mult).then_inc(ln_pool.sem[s], 1)

            def add_bias(s, g, layer):
                bias = B1 if layer == 1 else BL
                pool.wait_ge(res.sem[s], res.count(g, 1 if layer == 1 else 3))
                pool.tensor_tensor(RB[s][:], RES[s][:], bias[:].rearrange("p (o c) -> p o c", o=1)
                                   .broadcast_to([P, GB, C]), ALU.add).then_inc(rb.sem[s], 1)

            def do(part, s, g):
                kind, n = kind_of(part)
                if kind == "ln":
                    layernorm(s, g, n)
                elif kind == "bias":
                    add_bias(s, g, n)

            walk(pool, POOL_ORDER, do)

        @block.scalar
        def _(act):
            act.wait_ge(consts, 1)

            def copy(s, to, bank_n, done, led, g, part):
                act.wait_ge(led.sem[s], led.count(g, part))
                act.activation(to, bank[s][bank_n][:], ACT.Copy).then_inc(done.sem[s], 1)

            def gate(s, g, to, bank_n, led, part, which, scale, done):
                act.wait_ge(led.sem[s], led.count(g, part))
                for k in range(KB):
                    ins = act.activation(to[s][:, k, :], bank[s][bank_n][:, k, :], ACT.Tanh, scale=scale,
                                         bias=gate_bias[:, which, k:k + 1])
                ins.then_inc(done.sem[s], 1)

            def do(part, s, g):
                kind, n = kind_of(part)
                if kind == "norm":
                    src = X[s] if n == 0 else RES[s]
                    act.wait_ge(ln_pool.sem[s], ln_pool.count(g, 4 * n + 4))
                    for b in range(GB):
                        ins = act.activation(H[s][:, b, :], src[:, b, :], ACT.Relu,
                                             bias=nmr[s][:, b:b + 1], scale=rstd[s][:, b:b + 1])
                    ins.then_inc(h_ready.sem[s], 1)
                elif part == "h0_hi":
                    copy(s, HTh[s][:], 0, hT_hi, in_bank0, g, "turn0")
                elif part == "hT":
                    copy(s, HT[s][:], 0, hT_ready, in_bank0, g, "turn2")
                    copy(s, HTh[s][:], 0, hT_hi, in_bank0, g, "turn2")
                elif part == "hh":
                    copy(s, HH[s][:], 1, hh_ready, in_bank1, g, "project")
                    copy(s, HHh[s][:], 1, a_hi, in_bank1, g, "project")
                elif part == "exp_p":
                    act.wait_ge(soft.sem[s], soft.count(g, 6))
                    act.activation(E1[s][:, 0, :], E2[s][:, 0, :], ACT.Exp).then_inc(p_exp.sem[s], 1)
                elif part == "p_hi":
                    act.wait_ge(in_bank0.sem[s], in_bank0.count(g, "turn_p"))
                    act.activation(PTh[s][:, 0, :], bank[s][0][:, 0, :], ACT.Copy).then_inc(q_hi.sem[s], 1)
                elif part == "exp_v":
                    act.wait_ge(in_bank1.sem[s], in_bank1.count(g, "attend"))
                    act.activation(E1[s][:], bank[s][1][:], ACT.Exp).then_inc(elu_e.sem[s], 1)
                elif part in ("y1_hi", "y3_hi"):
                    copy(s, Ah[s][:], 0, a_hi, in_bank0, g, f"spread{part[1]}")
                elif kind == "natural":
                    copy(s, H[s][:], 1, h_back, in_bank1, g, f"back{n}")
                elif kind == "a_hi":
                    copy(s, Ah[s][:], 1, a_hi, in_bank1, g, f"a{n}")
                elif kind == "tz":
                    gate(s, g, TZ, 0, in_bank0, f"z{n}", 0, 0.5, z_ready)
                elif kind == "tr":
                    gate(s, g, TR, 0, in_bank0, f"r{n}", 1, 0.5, r_ready)
                elif kind == "q_hi":
                    act.wait_ge(q_ready.sem[s], q_ready.count(g, n + 1))
                    act.activation(QTh[s][:], QT[s][:], ACT.Copy).then_inc(q_hi.sem[s], 1)
                elif kind == "tc":
                    gate(s, g, HV, 1, in_bank1, f"c{n}", 2, 1.0, c_ready)
                elif kind == "h_hi":
                    act.wait_ge(hT_ready.sem[s], hT_ready.count(g, n + 1))
                    act.activation(HTh[s][:], HT[s][:], ACT.Copy).then_inc(hT_hi.sem[s], 1)

            walk(act, ACT_ORDER, do)

        @block.vector
        def _(dve):
            dve.wait_ge(const_in, 16 * len(loads))
            chain = [0]

            def link(ins):
                chain[0] += 1
                ins.then_inc(vchain, 1)
                dve.wait_ge(vchain, chain[0])

            link(dve.tensor_reduce(deg[:], A[:], AX.X, ALU.add))
            link(dve.tensor_scalar(deg_on[:], deg[:], 0.0, None, ALU.is_gt))
            link(dve.tensor_scalar(deg_lo[:], deg[:], TINY, None, ALU.max))
            dve.wait_ge(setup_pw, 1)
            link(dve.tensor_tensor(dis[:], deg_p[:], deg_on[:], ALU.mult))
            link(dve.tensor_scalar(adn[:], A[:], dis[:], None, ALU.mult))
            link(dve.tensor_copy(a2bc[:], acol[:, KB:2 * KB].rearrange("p (k o) -> p k o", o=1)
                                 .broadcast_to([P, KB, P])))
            link(dve.tensor_scalar(betaI[:], ident[:], beta_c[:], None, ALU.mult))
            link(dve.tensor_tensor(gate_sum[:, 0:2, :], gate_raw[:, 0:2, :],
                                   gate_raw[:, 3:4, :].broadcast_to([P, 2, KB]), ALU.add))
            link(dve.tensor_tensor(gate_sum[:, 2, :], gate_raw[:, 2, :], gate_raw[:, 4, :], ALU.add))
            link(dve.tensor_scalar(gate_bias[:, 0:2, :], gate_sum[:, 0:2, :], 0.5, None, ALU.mult))
            link(dve.tensor_copy(gate_bias[:, 2, :], gate_sum[:, 2, :]))

            def halves(k, src):
                link(dve.tensor_copy(hi[k][:], src))
                link(dve.tensor_tensor(lo[k][:], src, hi[k][:].bitcast(F32), ALU.subtract))

            link(dve.tensor_tensor(w3s[:], w3r[0][:], w3r[1][:], ALU.add))
            halves("Z", w3s[:])
            link(dve.tensor_tensor(w4s[:], w4r[0][:], w4r[1][:], ALU.add))
            link(dve.tensor_tensor(ws[:], w4s[:], w3s[:], ALU.subtract))
            halves("R", ws[:])
            link(dve.tensor_tensor(ws[:], w5r[0][:], w5r[1][:], ALU.add))
            halves("V", ws[:])
            halves("U", u3r[:])
            link(dve.tensor_scalar(ws[:], u5r[:], 0.5, None, ALU.mult))
            halves("UC", ws[:])
            halves("W0", w0r[:])
            halves("W1", w1r[:])
            halves("WL", wlr[:])
            dve.wait_ge(setup_pe, 1)
            link(dve.tensor_scalar(NT[:], bank[0][0][:, 0, 0:P], dis[:], None, ALU.mult))
            halves("WA2", bank[0][1][:, :, 0:P])
            dve.engine_nop().then_inc(consts, 1)

            def stats_of(s, g, layer):
                src = X[s] if layer == 0 else RES[s]
                if layer == 0:
                    dve.wait_ge(x_in.sem[s], x_in.count(g, 16))
                else:
                    dve.wait_ge(res.sem[s], res.count(g, layer))
                for b in range(GB):
                    ins = dve.bn_stats(stats[s][:, b, :], src[:, b, :])
                ins.then_inc(ln_mv.sem[s], 1)

            def aggregate(s, g, layer):
                dve.wait_ge(ln_mv.sem[s], ln_mv.count(g, 3 * layer + 1))
                dve.sem_inc(ln_mv.sem[s], 1)
                for b in range(GB):
                    ins = dve.bn_aggr(mv[s][:, b, :], stats[s][:, b, :])
                ins.then_inc(ln_mv.sem[s], 1)

            def by_graph(ap):
                return ap.rearrange("p (b m) -> p b m", m=P)

            def wide(col):
                return col[:].rearrange("p (b o) -> p b o", o=1).broadcast_to([P, GB, P])

            def soft_step(ins, s, g, n):
                ins.then_inc(soft.sem[s], 1)
                dve.wait_ge(soft.sem[s], soft.count(g, n))

            def node_scores(s, g):
                dve.wait_ge(hh_ready.sem[s], hh_ready.count(g, 1))
                for b in range(GB):
                    ins = dve.tensor_tensor_reduce(out=E2[s][:, b, :], in0=HH[s][:, b, :], in1=a1bc[:], scale=1.0,
                                                   scalar=0.0, op0=ALU.mult, op1=ALU.add,
                                                   accum_out=s1[s][:, b:b + 1])
                ins.then_inc(soft.sem[s], 1)

            def exponents(s, g):
                e1, e2 = by_graph(E1[s][:, 0, :]), by_graph(E2[s][:, 0, :])
                dve.wait_ge(soft.sem[s], soft.count(g, 1))
                dve.wait_ge(in_bank0.sem[s], in_bank0.count(g, "scores"))
                soft_step(dve.tensor_tensor(e1, by_graph(bank[s][0][:, 0, :]), wide(s1[s]), ALU.add), s, g, 2)
                soft_step(dve.scalar_tensor_tensor(e2, e1, SLOPE, e1, ALU.mult, ALU.max), s, g, 3)
                soft_step(dve.tensor_tensor(e1, e2, A[:].rearrange("p (o m) -> p o m", o=1)
                                            .broadcast_to([P, GB, P]), ALU.mult), s, g, 4)
                soft_step(dve.tensor_reduce(top[s][:], e1, AX.X, ALU.max), s, g, 5)
                dve.tensor_tensor(e2, e1, wide(top[s]), ALU.subtract).then_inc(soft.sem[s], 1)

            def probabilities(s, g):
                dve.wait_ge(p_exp.sem[s], p_exp.count(g, 1))
                soft_step(dve.tensor_reduce(tot[s][:], by_graph(E1[s][:, 0, :]), AX.X, ALU.add), s, g, 7)
                soft_step(dve.reciprocal(rtot[s][:], tot[s][:]), s, g, 8)
                for b in range(GB):
                    ins = dve.scalar_tensor_tensor(E2[s][:, 0, b * P:(b + 1) * P], E1[s][:, 0, b * P:(b + 1) * P],
                                                   rtot[s][:, b:b + 1], betaI[:], ALU.mult, ALU.add)
                ins.then_inc(p_beta.sem[s], 1)

            def attend(s, g):
                dve.wait_ge(elu_e.sem[s], elu_e.count(g, 1))
                dve.tensor_scalar(E2[s][:], E1[s][:], 1.0, -1.0, ALU.min, ALU.add).then_inc(elu_v.sem[s], 1)
                dve.wait_ge(elu_v.sem[s], elu_v.count(g, 1))
                dve.tensor_tensor(E1[s][:], bank[s][1][:], E2[s][:], ALU.max).then_inc(elu_v.sem[s], 1)
                dve.wait_ge(elu_v.sem[s], elu_v.count(g, 2))
                dve.tensor_tensor(RES[s][:], E1[s][:], X[s][:], ALU.add).then_inc(res.sem[s], 1)

            def low(s, g, out, whole, high, led, n, done):
                dve.wait_ge(led.sem[s], led.count(g, n))
                dve.tensor_tensor(out, whole, high.bitcast(F32), ALU.subtract).then_inc(done.sem[s], 1)

            def do(part, s, g):
                kind, n = kind_of(part)
                if kind == "stats":
                    stats_of(s, g, n)
                elif kind == "aggr":
                    aggregate(s, g, n)
                elif part == "h0_lo":
                    low(s, g, HTl[s][:], bank[s][0][:], HTh[s][:], hT_hi, 1, hT_lo)
                elif part == "hh_lo":
                    low(s, g, HHl[s][:], HH[s][:], HHh[s][:], a_hi, "project", a_lo)
                elif part == "s1":
                    node_scores(s, g)
                elif part == "soft_a":
                    exponents(s, g)
                elif part == "soft_b":
                    probabilities(s, g)
                elif part == "p_lo":
                    low(s, g, PTl[s][:, 0, :], bank[s][0][:, 0, :], PTh[s][:, 0, :], q_hi, "turn_p", q_lo)
                elif part == "elu":
                    attend(s, g)
                elif part in ("y1_lo", "y3_lo"):
                    low(s, g, Al[s][:], bank[s][0][:], Ah[s][:], a_hi, f"spread{part[1]}", a_lo)
                elif part == "x2":
                    dve.wait_ge(rb.sem[s], rb.count(g, 1))
                    dve.wait_ge(in_bank1.sem[s], in_bank1.count(g, "mix1"))
                    dve.tensor_tensor(RES[s][:], bank[s][1][:], RB[s][:], ALU.add).then_inc(res.sem[s], 1)
                elif part == "out":
                    dve.wait_ge(rb.sem[s], rb.count(g, 2))
                    dve.wait_ge(stored.sem[s], stored.count(g, 16))
                    dve.wait_ge(in_bank1.sem[s], in_bank1.count(g, "mix3"))
                    dve.tensor_tensor(OUT[s][:], bank[s][1][:], RB[s][:], ALU.add).then_inc(out_ready.sem[s], 1)
                elif kind == "h_lo":
                    low(s, g, HTl[s][:], HT[s][:], HTh[s][:], hT_hi, n + 2, hT_lo)
                elif kind == "a_lo":
                    low(s, g, Al[s][:], bank[s][1][:], Ah[s][:], a_hi, f"a{n}", a_lo)
                elif kind == "q":
                    dve.wait_ge(r_ready.sem[s], r_ready.count(g, n + 1))
                    dve.scalar_tensor_tensor(QT[s][:], TR[s][:], 1.0, HT[s][:], ALU.add, ALU.mult)\
                       .then_inc(q_ready.sem[s], 1)
                elif kind == "q_lo":
                    low(s, g, QTl[s][:], QT[s][:], QTh[s][:], q_hi, f"r{n}", q_lo)
                elif kind == "upd":
                    dve.wait_ge(c_ready.sem[s], c_ready.count(g, n + 1))
                    dve.tensor_tensor(QT[s][:], HV[s][:], HT[s][:], ALU.subtract).then_inc(upd.sem[s], 1)
                    dve.wait_ge(upd.sem[s], upd.count(g, 2 * n + 1))
                    dve.scalar_tensor_tensor(HV[s][:], TZ[s][:], 1.0, QT[s][:], ALU.add, ALU.mult)\
                       .then_inc(upd.sem[s], 1)
                    dve.wait_ge(upd.sem[s], upd.count(g, 2 * n + 2))
                    dve.scalar_tensor_tensor(HT[s][:], HV[s][:], 0.5, HT[s][:], ALU.mult, ALU.add)\
                       .then_inc(hT_ready.sem[s], 1)
                elif part == "x3":
                    dve.wait_ge(in_bank1.sem[s], in_bank1.count(g, f"back{T}"))
                    dve.tensor_tensor(RES[s][:], bank[s][1][:], RES[s][:], ALU.add).then_inc(res.sem[s], 1)

            walk(dve, DVE_ORDER, do)

        @block.tensor
        def _(pe):
            pe.wait_ge(const_in, 16 * len(loads))
            pe.wait_ge(vchain, 6)
            pe.transpose(bank[0][0][:, 0, 0:P], adn[:], ident[:])
            for c in range(KB):
                for k in range(KB):
                    ins = pe.matmul(bank[0][1][:, c, 0:P], W0T[:, k, c * P:(c + 1) * P], a2bc[:, k, :],
                                    start=(k == 0), stop=(k == KB - 1))
            ins.then_inc(setup_pe, 1)
            pe.wait_ge(consts, 1)

            def turn(s, done):
                for k in range(KB):
                    for b in range(GB):
                        ins = pe.transpose(bank[s][0][:, k, b * P:(b + 1) * P], H[s][:, b, k * P:(k + 1) * P], ident[:])
                ins.then_inc(done.sem[s], 1)

            def back(s, done):
                for b in range(GB):
                    for k in range(KB):
                        ins = pe.transpose(bank[s][1][:, b, k * P:(k + 1) * P], HT[s][:, k, b * P:(b + 1) * P], ident[:])
                ins.then_inc(done.sem[s], 1)

            def spread(s, to, right, done):
                for k in range(KB):
                    for b in range(GB):
                        ins = pe.matmul(bank[s][to][:, k, b * P:(b + 1) * P], H[s][:, b, k * P:(k + 1) * P],
                                        right[:], start=True, stop=True)
                ins.then_inc(done.sem[s], 1)

            def rows(s, g, left_hi, left_lo, key, low_ready, low_n, done):
                for b in range(GB):
                    n = 0
                    for left, wk in ((left_hi, hi), (left_hi, lo), (left_lo, hi)):
                        if b == 0 and left is left_lo:
                            pe.wait_ge(low_ready.sem[s], low_ready.count(g, low_n))
                        for k in range(KB):
                            ins = pe.matmul(bank[s][1][:, b, :], left[s][:, k, b * P:(b + 1) * P], wk[key][:, k, :],
                                            start=(n == 0), stop=(n == 3 * KB - 1))
                            n += 1
                ins.then_inc(done.sem[s], 1)

            def gate(s, g, key, right_hi, right_lo, to, opens, closes, low_ready, low_n, done):
                for o in range(KB):
                    n = 0
                    for wk, right in ((hi, right_hi), (lo, right_hi), (hi, right_lo)):
                        if o == 0 and right is right_lo:
                            pe.wait_ge(low_ready.sem[s], low_ready.count(g, low_n))
                        for k in range(KB):
                            ins = pe.matmul(bank[s][to][:, o, :], wk[key][:, k, o * P:(o + 1) * P], right[s][:, k, :],
                                            start=(opens and o == 0 and n == 0), stop=(closes and n == 3 * KB - 1),
                                            skip_group_check=True)
                            n += 1
                if done is not None:
                    ins.then_inc(done.sem[s], 1)

            def do(part, s, g):
                kind, n = kind_of(part)
                if part == "turn0":
                    pe.wait_ge(h_ready.sem[s], h_ready.count(g, 1))
                    turn(s, in_bank0)
                elif kind == "project":
                    pe.wait_ge(hT_hi.sem[s], hT_hi.count(g, 1))
                    rows(s, g, HTh, HTl, "W0", hT_lo, 1, in_bank1)
                elif kind == "scores":
                    n = 0
                    for wk, right in ((hi, HTh), (lo, HTh), (hi, HTl)):
                        for k in range(KB):
                            ins = pe.matmul(bank[s][0][:, 0, :], wk["WA2"][:, k, :], right[s][:, k, :],
                                            start=(n == 0), stop=(n == 3 * KB - 1))
                            n += 1
                    ins.then_inc(in_bank0.sem[s], 1)
                elif kind == "turn_p":
                    pe.wait_ge(p_beta.sem[s], p_beta.count(g, 1))
                    for b in range(GB):
                        ins = pe.transpose(bank[s][0][:, 0, b * P:(b + 1) * P], E2[s][:, 0, b * P:(b + 1) * P], ident[:])
                    ins.then_inc(in_bank0.sem[s], 1)
                elif kind == "attend":
                    pe.wait_ge(a_lo.sem[s], a_lo.count(g, "project"))
                    pe.wait_ge(q_lo.sem[s], q_lo.count(g, "turn_p"))
                    for b in range(GB):
                        n = 0
                        for left, right in ((PTh, HHh), (PTh, HHl), (PTl, HHh)):
                            ins = pe.matmul(bank[s][1][:, b, :], left[s][:, 0, b * P:(b + 1) * P], right[s][:, b, :],
                                            start=(n == 0), stop=(n == 2))
                            n += 1
                    ins.then_inc(in_bank1.sem[s], 1)
                elif kind == "spread":
                    pe.wait_ge(h_ready.sem[s], h_ready.count(g, 2 if n == 1 else 4))
                    spread(s, 0, NT if n == 1 else AT, in_bank0)
                elif kind == "mix":
                    pe.wait_ge(a_hi.sem[s], a_hi.count(g, f"spread{n}"))
                    rows(s, g, Ah, Al, "W1" if n == 1 else "WL", a_lo, f"spread{n}", in_bank1)
                elif part == "turn2":
                    pe.wait_ge(h_ready.sem[s], h_ready.count(g, 3))
                    turn(s, in_bank0)
                elif kind == "back":
                    pe.wait_ge(hT_ready.sem[s], hT_ready.count(g, 1 + n))
                    back(s, in_bank1)
                elif kind == "u":
                    pe.wait_ge(hT_hi.sem[s], hT_hi.count(g, n + 2))
                    gate(s, g, "U", HTh, HTl, 0, True, False, hT_lo, n + 2, None)
                elif kind == "a":
                    if n:
                        pe.wait_ge(h_back.sem[s], h_back.count(g, n))
                    spread(s, 1, AT, in_bank1)
                elif kind == "z":
                    pe.wait_ge(a_hi.sem[s], a_hi.count(g, f"a{n}"))
                    gate(s, g, "Z", Ah, Al, 0, False, True, a_lo, f"a{n}", in_bank0)
                elif kind == "v":
                    gate(s, g, "V", Ah, Al, 1, True, False, a_lo, f"a{n}", None)
                elif kind == "r":
                    pe.wait_ge(z_ready.sem[s], z_ready.count(g, n + 1))
                    gate(s, g, "R", Ah, Al, 0, False, True, a_lo, f"a{n}", in_bank0)
                elif kind == "c":
                    pe.wait_ge(q_hi.sem[s], q_hi.count(g, f"r{n}"))
                    gate(s, g, "UC", QTh, QTl, 1, False, True, q_lo, f"r{n}", in_bank1)

            walk(pe, PE_ORDER, do)


def kernel(x, adj, L0_gnn_W, L0_gnn_a, L0_gnn_beta, L1_gnn_weight, L1_gnn_bias, L2_gnn_w3_w, L2_gnn_w3_b,
           L2_gnn_u3_w, L2_gnn_u3_b, L2_gnn_w4_w, L2_gnn_w4_b, L2_gnn_w5_w, L2_gnn_w5_b, L2_gnn_u5_w,
           L2_gnn_u5_b, L3_gnn_weight, L3_gnn_bias):
    import numpy as np
    import concourse.bacc as bacc
    from concourse.bass_utils import run_bass_kernel_spmd

    def rows(v):
        return np.broadcast_to(np.asarray(v)[None, :], (P, C))

    def blocks(v):
        return np.asarray(v).reshape(KB, P).T

    host = {
        "x": x,
        "adj": adj,
        "adjT": np.asarray(adj).T,
        "ident": np.eye(P, dtype=np.float32),
        "w0": L0_gnn_W,
        "w0T": np.asarray(L0_gnn_W).T,
        "a_cols": np.asarray(L0_gnn_a).reshape(2 * KB, P).T,
        "a1_rows": rows(np.asarray(L0_gnn_a)[0:C, 0]),
        "beta": np.broadcast_to(np.asarray(L0_gnn_beta)[None, :], (P, 1)),
        "w1": L1_gnn_weight,
        "b1": rows(L1_gnn_bias),
        "w3T": np.asarray(L2_gnn_w3_w).T,
        "w4T": np.asarray(L2_gnn_w4_w).T,
        "w5T": np.asarray(L2_gnn_w5_w).T,
        "u3T": np.asarray(L2_gnn_u3_w).T,
        "u5T": np.asarray(L2_gnn_u5_w).T,
        "gate_b": np.stack([blocks(v) for v in (L2_gnn_w3_b, L2_gnn_w4_b, L2_gnn_w5_b, L2_gnn_u3_b, L2_gnn_u5_b)], axis=1),
        "wl": L3_gnn_weight,
        "bl": rows(L3_gnn_bias),
    }
    host = {k: np.ascontiguousarray(v) for k, v in host.items()}
    nc = bacc.Bacc("TRN2", target_bir_lowering=False, num_devices=1)
    args = [nc.dram_tensor(k + "_dram", v.shape, mybir.dt.from_np(v.dtype), kind="ExternalInput").ap() for k, v in host.items()]
    args.append(nc.dram_tensor("out_dram", (B, P, C), F32, kind="ExternalOutput").ap())
    build(nc, *args)
    r = run_bass_kernel_spmd(nc, [{k + "_dram": v for k, v in host.items()}], core_ids=[0])
    return r.results[0]["out_dram"]
```

```python
import concourse.bass as bass
from concourse import mybir
from contextlib import ExitStack

F32 = mybir.dt.float32
F32R = mybir.dt.float32r
ALU = mybir.AluOpType
ACT = mybir.ActivationFunctionType
AX = mybir.AxisListType

P = 128
C = 256
KB = C // P
B = 64
GB = 2
NS = 4
NG = B // GB // NS
W = GB * P
T = 3
EPS = 1e-5
SLOPE = 0.2
TINY = 1.1754943508222875e-38

PE_START = """
    w0a_sum:0 s2_rows:0 turn_p:0 turn_adn:0 spread0:0 mix0:0 s2_rows:1 spread1:0 mix1:0 turn_p:1
    spread0:1 turn2:0 a0:0 u0:0 z0:0 mix0:1 r0:0 v0:0 c0:0 s2_rows:2 spread1:1 back1:0 mix1:1 a1:0 u1:0
    z1:0 v1:0 turn2:1 r1:0 a0:1 turn_p:2 u0:1 spread0:2 c1:0 mix0:2 z0:1 back2:0 r0:1 v0:1 a2:0 u2:0
    c0:1
"""
PE_STEADY = """
    z2:3 spread1:1 v2:3 r2:3 mix1:1 back1:2 u1:2 a1:2 s2_rows:0 c2:3 z1:2 turn2:1 v1:2 r1:2 u0:1 back3:3
    turn_p:0 a0:1 spread0:0 c1:2 z0:1 mix0:0 v0:1 r0:1 spread3:3 back2:2 u2:2 a2:2 mix3:3 c0:1
"""
PE_END = """
    spread1:2 z2:0 mix1:2 v2:0 back1:1 r2:0 a1:1 u1:1 s2_rows:3 z1:1 c2:0 turn2:2 a0:2 r1:1 v1:1 back3:0
    turn_p:3 u0:2 spread0:3 c1:1 z0:2 mix0:3 r0:2 back2:1 v0:2 u2:1 a2:1 c0:2 z2:1 v2:1 spread1:3 r2:1
    mix1:3 back1:2 spread3:0 a1:2 u1:2 z1:2 turn2:3 a0:3 r1:2 v1:2 u0:3 mix3:0 c1:2 z0:3 c2:1 r0:3
    back2:2 u2:2 a2:2 v0:3 z2:2 c0:3 back3:1 r2:2 v2:2 back1:3 a1:3 c2:2 u1:3 z1:3 back3:2 r1:3
    spread3:1 v1:3 c1:3 mix3:1 back2:3 spread3:2 a2:3 u2:3 z2:3 r2:3 mix3:2 v2:3 c2:3 back3:3 spread3:3
    mix3:3
"""
ACT_START = """
    norm0:0 exp_p:0 pt:0 y_hi0:0 exp_v:0 norm0:1 norm1:0 y_hi1:0 exp_p:1 pt:1 norm2:0 y_hi0:1 hT:0
    a_hi0:0 tz0:0 exp_v:1 tr0:0 q_hi0:0 norm0:2 tc0:0 norm1:1 y_hi1:1 h_hi1:0 natural1:0 a_hi1:0 norm2:1
    tz1:0 exp_p:2 hT:1 tr1:0 pt:2 q_hi1:0 a_hi0:1 y_hi0:2 tc1:0 exp_v:2 tz0:1 natural2:0 h_hi2:0 tr0:1
    q_hi0:1 a_hi2:0 norm1:2
"""
ACT_STEADY = """
    tc0:2 tz2:3 norm0:0 y_hi1:1 h_hi1:2 tr2:3 natural1:2 q_hi2:3 a_hi1:2 norm2:1 tc2:3 tz1:2 hT:1
    exp_p:0 tr1:2 pt:0 q_hi1:2 a_hi0:1 y_hi0:0 tc1:2 tz0:1 exp_v:0 norm3:3 h_hi2:2 tr0:1 y_hi3:3
    natural2:2 q_hi0:1 a_hi2:2 norm1:0
"""
ACT_END = """
    tc0:1 y_hi1:2 tz2:0 norm0:3 h_hi1:1 natural1:1 tr2:0 a_hi1:1 q_hi2:0 norm2:2 tz1:1 tc2:0 hT:2
    exp_p:3 tr1:1 pt:3 q_hi1:1 a_hi0:2 y_hi0:3 tc1:1 tz0:2 exp_v:3 h_hi2:1 tr0:2 natural2:1 q_hi0:2
    a_hi2:1 tc0:2 norm1:3 tz2:1 h_hi1:2 y_hi1:3 norm3:0 tr2:1 natural1:2 a_hi1:2 y_hi3:0 norm2:3 q_hi2:1
    tz1:2 hT:3 a_hi0:3 tr1:2 q_hi1:2 tc1:2 tz0:3 tc2:1 h_hi2:2 tr0:3 natural2:2 q_hi0:3 a_hi2:2 tz2:2
    tc0:3 tr2:2 h_hi1:3 natural1:3 q_hi2:2 a_hi1:3 tc2:2 tz1:3 norm3:1 tr1:3 q_hi1:3 y_hi3:1 tc1:3
    norm3:2 h_hi2:3 natural2:3 a_hi2:3 tz2:3 y_hi3:2 tr2:3 q_hi2:3 tc2:3 norm3:3 y_hi3:3
"""
DVE_START = """
    a_bc:0 stats0:0 deg:0 aggr0:0 adn:0 w0a:0 node:0 soft_a:0 stats0:1 soft_b:0 U:0 W1:0 aggr0:1 W0:0
    NT:0 y_lo0:0 V:0 elu:0 stats1:0 aggr1:0 node:1 Z:0 soft_a:1 y_lo1:0 soft_b:1 stats0:2 x2:0 stats2:0
    aggr2:0 gate_bias:0 aggr0:2 UC:0 y_lo0:1 h_lo0:0 a_lo0:0 R:0 elu:1 q0:0 stats1:1 aggr1:1 q_lo0:0
    node:2 upd0:0 y_lo1:1 h_lo1:0 x2:1 stats2:1 aggr2:1 a_lo1:0 soft_a:2 soft_b:2 h_lo0:1 q1:0 q_lo1:0
    y_lo0:2 a_lo0:1 upd1:0 elu:2 stats1:2 aggr1:2 q0:1 h_lo2:0 WL:0 q_lo0:1 a_lo2:0
"""
DVE_STEADY = """
    stats0:0 aggr0:0 upd0:2 y_lo1:1 node:0 h_lo1:2 x2:1 q2:3 stats2:1 aggr2:1 q_lo2:3 a_lo1:2 soft_a:0
    upd2:3 h_lo0:1 soft_b:0 q1:2 x3:3 q_lo1:2 stats3:3 a_lo0:1 y_lo0:0 aggr3:3 upd1:2 elu:0 h_lo2:2
    stats1:0 q0:1 y_lo3:3 aggr1:0 q_lo0:1 a_lo2:2 out:3
"""
DVE_END = """
    stats0:3 aggr0:3 y_lo1:2 upd0:1 x2:2 node:3 h_lo1:1 stats2:2 aggr2:2 q2:0 a_lo1:1 q_lo2:0 soft_a:3
    upd2:0 soft_b:3 h_lo0:2 q1:1 q_lo1:1 a_lo0:2 y_lo0:3 upd1:1 elu:3 h_lo2:1 q0:2 x3:0 stats1:3 q_lo0:2
    aggr1:3 a_lo2:1 stats3:0 upd0:2 aggr3:0 y_lo1:3 h_lo1:2 x2:3 stats2:3 aggr2:3 q2:1 a_lo1:2 y_lo3:0
    q_lo2:1 h_lo0:3 q1:2 q_lo1:2 a_lo0:3 upd1:2 h_lo2:2 q0:3 q_lo0:3 a_lo2:2 upd2:1 upd0:3 x3:1 q2:2
    h_lo1:3 stats3:1 q_lo2:2 aggr3:1 out:0 a_lo1:3 upd2:2 x3:2 stats3:2 aggr3:2 q1:3 q_lo1:3 y_lo3:1
    upd1:3 h_lo2:3 a_lo2:3 y_lo3:2 out:1 q2:3 out:2 q_lo2:3 upd2:3 x3:3 stats3:3 aggr3:3 y_lo3:3 out:3
"""
POOL_START = """
    ln0:0 pow:0 ln0:1 ln1:0 bias1:0 ln2:0 ln0:2 ln1:1 bias1:1 ln2:1 ln1:2
"""
POOL_STEADY = """
    ln0:0 bias1:1 ln2:1 ln3:3 bias3:3 ln1:0
"""
POOL_END = """
    ln0:3 bias1:2 ln2:2 bias1:3 ln1:3 bias3:0 ln3:0 ln2:3 ln3:1 bias3:2 ln3:2 bias3:1 ln3:3 bias3:3
"""
SP_START = ""
SP_STEADY = f"load:{NS - 1} store:{NS - 1}"
SP_END = " ".join(f"store:{n}" for n in range(NS))


def parts(order):
    return [(p.split(":")[0], int(p.split(":")[1])) for p in order.split()]


def kind_of(part):
    kind = part.rstrip("0123456789")
    return kind, int("0" + part[len(kind):])


def walk(engine, start, steady, end, do):
    lead = NS - 1
    for part, group in parts(start):
        do(part, group, 0)
    with engine.Fori(0, NG - 1) as i:
        for q in range(lead, lead + NS):
            for part, ago in parts(steady):
                later = (q - ago) // NS
                do(part, (q - ago) % NS, i + later if later else i)
    for part, stream in parts(end):
        do(part, stream, NG - 1)


class Awaited:

    def __init__(self):
        self.names = set()

    def new(self, name):
        if name in self.names:
            return False
        self.names.add(name)
        return True


class Signal:

    def __init__(self, ctx, nc, name, events):
        self.sem = [ctx.enter_context(nc.semaphore(f"{name}_{s}")) for s in range(NS)]
        self.events = None if type(events) is int else events
        self.per_group = events if type(events) is int else len(events)

    def count(self, g, n):
        return g * self.per_group + (n if self.events is None else self.events.index(n) + 1)


SMALL = {"ident": P, "adj": P, "adjT": P, "a": 2 * KB, "beta": 1, "gate_bias": 5 * KB}
ROWS = {"b1": C, "bl": C}


def columns(sizes, name):
    names = list(sizes)
    at = sum(sizes[k] for k in names[:names.index(name)])
    return slice(at, at + sizes[name])


def build(nc, x, small_in, rows_in, w0, w0T, w1, w3T, w4T, w5T, u3T, u5T, wl, out):
    with ExitStack() as ctx:
        def sb(name, shape, dt=F32):
            return ctx.enter_context(nc.sbuf_tensor(name, shape, dt))

        def sem(name):
            return ctx.enter_context(nc.semaphore(name))

        def signal(name, per_group):
            return Signal(ctx, nc, name, per_group)

        def per_stream(name, shape, dt=F32):
            return [sb(f"{name}_{s}", shape, dt) for s in range(NS)]

        small = sb("small", [P, sum(SMALL.values())])
        rows_c = sb("rows_c", [P, sum(ROWS.values())])
        ident = small[:, columns(SMALL, "ident")]
        A = small[:, columns(SMALL, "adj")]
        AT = small[:, columns(SMALL, "adjT")]
        a_cols = small[:, columns(SMALL, "a")]
        beta_c = small[:, columns(SMALL, "beta")]
        gate_raw = small[:, columns(SMALL, "gate_bias")].rearrange("p (j k) -> p j k", k=KB)
        B1 = rows_c[:, columns(ROWS, "b1")]
        BL = rows_c[:, columns(ROWS, "bl")]
        NT = sb("NT", [P, P])
        betaI = sb("betaI", [P, P])
        W0T = sb("W0T", [P, KB, C])
        a_bc = sb("a_bc", [P, 2 * KB, P])
        W0a = sb("W0a", [P, 2, C])
        gate_sum = sb("gate_sum", [P, 3, KB])
        gate_bias = sb("gate_bias", [P, 3, KB])
        deg = sb("deg", [P, 1])
        deg_on = sb("deg_on", [P, 1])
        deg_lo = sb("deg_lo", [P, 1])
        deg_p = sb("deg_p", [P, 1])
        dis = sb("dis", [P, 1])
        half = sb("half", [P, GB])
        eps = sb("eps", [P, GB])
        minus = sb("minus", [P, GB])
        adn = sb("adn", [P, P])
        weights = ["Z", "R", "V", "U", "UC", "W0", "W1", "WL"]
        hi = {k: sb(f"{k}hi", [P, KB, C], F32R) for k in weights}
        lo = {k: sb(f"{k}lo", [P, KB, C], F32R) for k in weights}

        X = per_stream("X", [P, GB, C])
        RES = per_stream("RES", [P, GB, C])
        RB = per_stream("RB", [P, GB, C])
        OUT = per_stream("OUT", [P, GB, C])
        H = per_stream("H", [P, GB, C])
        HT = per_stream("HT", [P, KB, W])
        HTh = per_stream("HTh", [P, KB, W], F32R)
        HTl = per_stream("HTl", [P, KB, W], F32R)
        Ah = per_stream("Ah", [P, KB, W], F32R)
        Al = per_stream("Al", [P, KB, W], F32R)
        QT = per_stream("QT", [P, KB, W])
        QTh = per_stream("QTh", [P, KB, W], F32R)
        QTl = per_stream("QTl", [P, KB, W], F32R)
        TZ = per_stream("TZ", [P, KB, W])
        TR = per_stream("TR", [P, KB, W])
        HV = TR
        PT = TZ
        E1, E2 = TR, QT
        stats = per_stream("stats", [P, GB, 6])
        mv = per_stream("mv", [P, GB, 2])
        ve = per_stream("ve", [P, GB])
        rstd = per_stream("rstd", [P, GB])
        mr = per_stream("mr", [P, GB])
        nmr = per_stream("nmr", [P, GB])
        s1 = per_stream("s1", [P, GB])
        s2 = per_stream("s2", [P, GB])
        top = per_stream("top", [P, GB])
        tot = per_stream("tot", [P, GB])
        rtot = per_stream("rtot", [P, GB])

        raw = {n: sb(f"{n}_raw", [P, (2 if n in ("w3", "w4", "w5") else 1) * KB, C])
               for n in ("w0", "w1", "wl", "u3", "u5", "w3", "w4", "w5")}
        w3s, w4s, w5s, w43, u5h = (sb(n, [P, KB, C]) for n in ("w3s", "w4s", "w5s", "w43", "u5h"))

        bank = [[ctx.enter_context(nc.psum_tensor(f"bank{s}{k}", [P, KB, W], F32)) for k in range(2)]
                for s in range(NS)]

        loads = ["small", "w0T", "w0", "rows", "w1", "u3", "w3", "w5", "w4", "u5", "wl"]
        loaded = {n: sem(f"loaded_{n}") for n in loads}
        CONSTS = [p for p, _ in parts(DVE_START) if p in ("a_bc", "w0a", "deg", "adn", "NT", "gate_bias", *weights)]
        consts = sem("consts")
        const_step = sem("const_step")
        w0a_sum = sem("w0a_sum")
        adn_turned = sem("adn_turned")
        pool_set = sem("pool_set")
        deg_pow = sem("deg_pow")
        x_in = signal("x_in", 16)
        stored = signal("stored", 16)
        ln_mv = signal("ln_mv", 3 * 4)
        ln_pool = signal("ln_pool", 4 * 4)
        h_ready = signal("h_ready", 4)
        in_bank0 = signal("in_bank0", ["s2_rows", "turn_p", "spread0", "spread1", "turn2"]
                          + [f"{k}{t}" for t in range(T) for k in "zr"] + ["spread3"])
        in_bank1 = signal("in_bank1", ["mix0", "mix1"]
                          + [k for t in range(T) for k in (f"a{t}", f"c{t}", f"back{t + 1}")] + ["mix3"])
        hT_ready = signal("hT_ready", 1 + T)
        pt_ready = signal("pt_ready", 1)
        soft = signal("soft", 9)
        p_exp = signal("p_exp", 1)
        p_beta = signal("p_beta", 1)
        elu_e = signal("elu_e", 1)
        elu_v = signal("elu_v", 2)
        res = signal("res", 3)
        rb = signal("rb", 2)
        out_ready = signal("out_ready", 1)
        h_back = signal("h_back", T - 1)
        hT_hi = signal("hT_hi", T)
        hT_lo = signal("hT_lo", T)
        a_hi = signal("a_hi", ["spread0", "spread1"] + [f"a{t}" for t in range(T)] + ["spread3"])
        a_lo = signal("a_lo", a_hi.events)
        z_ready = signal("z_ready", T)
        r_ready = signal("r_ready", T)
        q_ready = signal("q_ready", T)
        q_hi = signal("q_hi", [f"r{t}" for t in range(T)])
        q_lo = signal("q_lo", q_hi.events)
        c_ready = signal("c_ready", T)
        upd = signal("upd", 2 * T)

        block = ctx.enter_context(nc.Block())

        def by_block(w):
            return w.rearrange("(k p) n -> p k n", p=P)

        sources = {"small": (small[:], small_in), "rows": (rows_c[:], rows_in), "w0T": (W0T[:], by_block(w0T))}
        for n, w in (("w0", w0), ("w1", w1), ("wl", wl), ("w3", w3T), ("w4", w4T), ("w5", w5T), ("u3", u3T),
                     ("u5", u5T)):
            sources[n] = (raw[n][:], by_block(w))

        def made(name):
            return CONSTS.index(name) + 1

        x_g = x.rearrange("(g b) n c -> g n b c", b=GB)
        out_g = out.rearrange("(g b) n c -> g n b c", b=GB)

        def group(dram, i):
            return dram[i] if type(i) is int else dram[bass.ds(i, 1)].rearrange("g n b c -> (g n) b c")

        @block.sync
        def _(sp):
            sp.dma_start(*sources[loads[0]]).then_inc(loaded[loads[0]], 16)
            sp.dma_start(X[0][:], x_g[0]).then_inc(x_in.sem[0], 16)
            for n in loads[1:]:
                sp.dma_start(*sources[n]).then_inc(loaded[n], 16)
                if n == "w0":
                    sp.dma_start(X[1][:], x_g[1]).then_inc(x_in.sem[1], 16)
            for s in range(NS):
                sp.sem_inc(stored.sem[s], 16)
            for s in range(2, NS):
                sp.dma_start(X[s][:], x_g[s]).then_inc(x_in.sem[s], 16)

            def do(part, s, g):
                if part == "load":
                    sp.wait_ge(res.sem[s], res.count(g, 1))
                    sp.dma_start(X[s][:], group(x_g, NS * g + NS + s)).then_inc(x_in.sem[s], 16)
                if part == "store":
                    sp.wait_ge(out_ready.sem[s], out_ready.count(g, 1))
                    sp.dma_start(group(out_g, NS * g + s), OUT[s][:]).then_inc(stored.sem[s], 16)

            walk(sp, SP_START, SP_STEADY, SP_END, do)
            for s in range(NS):
                sp.wait_ge(stored.sem[s], stored.count(NG, 16))

        @block.gpsimd
        def _(pool):
            pool.memset(half[:], -0.5).then_inc(pool_set, 1)
            pool.memset(eps[:], EPS).then_inc(pool_set, 1)
            pool.memset(minus[:], -1.0).then_inc(pool_set, 1)
            pool.wait_ge(pool_set, 3)
            awaited = Awaited()

            def layernorm(s, g, layer):
                n = 4 * layer
                pool.wait_ge(ln_mv.sem[s], ln_mv.count(g, 3 * layer + 3))
                pool.tensor_tensor(ve[s][:], mv[s][:, :, 1], eps[:], ALU.add).then_inc(ln_pool.sem[s], 1)
                pool.wait_ge(ln_pool.sem[s], ln_pool.count(g, n + 1))
                pool.tensor_tensor(rstd[s][:], ve[s][:], half[:], ALU.pow).then_inc(ln_pool.sem[s], 1)
                pool.wait_ge(ln_pool.sem[s], ln_pool.count(g, n + 2))
                pool.tensor_tensor(mr[s][:], mv[s][:, :, 0], rstd[s][:], ALU.mult).then_inc(ln_pool.sem[s], 1)
                pool.wait_ge(ln_pool.sem[s], ln_pool.count(g, n + 3))
                pool.tensor_tensor(nmr[s][:], mr[s][:], minus[:], ALU.mult).then_inc(ln_pool.sem[s], 1)

            def add_bias(s, g, layer):
                bias = B1 if layer == 1 else BL
                pool.wait_ge(res.sem[s], res.count(g, 1 if layer == 1 else 3))
                pool.tensor_tensor(RB[s][:], RES[s][:], bias[:].rearrange("p (o c) -> p o c", o=1)
                                   .broadcast_to([P, GB, C]), ALU.add).then_inc(rb.sem[s], 1)

            def do(part, s, g):
                kind, n = kind_of(part)
                if kind == "ln":
                    layernorm(s, g, n)
                elif part == "pow":
                    pool.wait_ge(consts, made("deg"))
                    pool.tensor_tensor(deg_p[:], deg_lo[:], half[:, 0:1], ALU.pow).then_inc(deg_pow, 1)
                elif kind == "bias":
                    if awaited.new("rows"):
                        pool.wait_ge(loaded["rows"], 16)
                    add_bias(s, g, n)

            walk(pool, POOL_START, POOL_STEADY, POOL_END, do)

        @block.scalar
        def _(act):
            awaited = Awaited()

            def copy(s, to, bank_n, done, led, g, part):
                act.wait_ge(led.sem[s], led.count(g, part))
                act.activation(to, bank[s][bank_n][:], ACT.Copy).then_inc(done.sem[s], 1)

            def gate(s, g, to, bank_n, led, part, which, scale, done):
                act.wait_ge(led.sem[s], led.count(g, part))
                for k in range(KB):
                    ins = act.activation(to[s][:, k, :], bank[s][bank_n][:, k, :], ACT.Tanh, scale=scale,
                                         bias=gate_bias[:, which, k:k + 1])
                ins.then_inc(done.sem[s], 1)

            def do(part, s, g):
                kind, n = kind_of(part)
                if kind == "norm":
                    src = X[s] if n == 0 else RES[s]
                    act.wait_ge(ln_pool.sem[s], ln_pool.count(g, 4 * n + 4))
                    for b in range(GB):
                        ins = act.activation(H[s][:, b, :], src[:, b, :], ACT.Relu,
                                             bias=nmr[s][:, b:b + 1], scale=rstd[s][:, b:b + 1])
                    ins.then_inc(h_ready.sem[s], 1)
                elif part == "hT":
                    copy(s, HT[s][:], 0, hT_ready, in_bank0, g, "turn2")
                    copy(s, HTh[s][:], 0, hT_hi, in_bank0, g, "turn2")
                elif part == "exp_p":
                    act.wait_ge(soft.sem[s], soft.count(g, 7))
                    act.activation(E1[s][:, 0, :], E2[s][:, 0, :], ACT.Exp).then_inc(p_exp.sem[s], 1)
                elif part == "pt":
                    act.wait_ge(in_bank0.sem[s], in_bank0.count(g, "turn_p"))
                    act.activation(PT[s][:, 0, :], bank[s][0][:, 0, :], ACT.Copy).then_inc(pt_ready.sem[s], 1)
                elif part == "exp_v":
                    act.wait_ge(in_bank1.sem[s], in_bank1.count(g, "mix0"))
                    act.activation(E1[s][:], bank[s][1][:], ACT.Exp).then_inc(elu_e.sem[s], 1)
                elif kind == "y_hi":
                    copy(s, Ah[s][:], 0, a_hi, in_bank0, g, f"spread{n}")
                elif kind == "natural":
                    copy(s, H[s][:], 1, h_back, in_bank1, g, f"back{n}")
                elif kind == "a_hi":
                    copy(s, Ah[s][:], 1, a_hi, in_bank1, g, f"a{n}")
                elif kind == "tz":
                    if awaited.new("gate_bias"):
                        act.wait_ge(consts, made("gate_bias"))
                    gate(s, g, TZ, 0, in_bank0, f"z{n}", 0, 0.5, z_ready)
                elif kind == "tr":
                    gate(s, g, TR, 0, in_bank0, f"r{n}", 1, 0.5, r_ready)
                elif kind == "q_hi":
                    act.wait_ge(q_ready.sem[s], q_ready.count(g, n + 1))
                    act.activation(QTh[s][:], QT[s][:], ACT.Copy).then_inc(q_hi.sem[s], 1)
                elif kind == "tc":
                    gate(s, g, HV, 1, in_bank1, f"c{n}", 2, 1.0, c_ready)
                elif kind == "h_hi":
                    act.wait_ge(hT_ready.sem[s], hT_ready.count(g, n + 1))
                    act.activation(HTh[s][:], HT[s][:], ACT.Copy).then_inc(hT_hi.sem[s], 1)

            walk(act, ACT_START, ACT_STEADY, ACT_END, do)

        @block.vector
        def _(dve):
            chain = [0]

            def link(ins):
                chain[0] += 1
                ins.then_inc(const_step, 1)
                dve.wait_ge(const_step, chain[0])

            load_of = {"a_bc": "small", "deg": "small", "gate_bias": "small", "W0": "w0", "W1": "w1", "U": "u3",
                       "Z": "w3", "V": "w5", "R": "w4", "UC": "u5", "WL": "wl"}

            def halves(key, src):
                link(dve.tensor_copy(hi[key][:], src))
                dve.tensor_tensor(lo[key][:], src, hi[key][:].bitcast(F32), ALU.subtract).then_inc(consts, 1)

            def both(total, key):
                link(dve.tensor_tensor(total[:], raw[key][:, 0:KB, :], raw[key][:, KB:2 * KB, :], ALU.add))

            def constant(name):
                if name in load_of:
                    dve.wait_ge(loaded[load_of[name]], 16)
                if name == "a_bc":
                    dve.tensor_copy(a_bc[:], a_cols.rearrange("p (k o) -> p k o", o=1)
                                    .broadcast_to([P, 2 * KB, P])).then_inc(consts, 1)
                elif name == "w0a":
                    dve.wait_ge(w0a_sum, 1)
                    link(dve.tensor_copy(W0a[:], bank[NS - 1][1][:]))
                    dve.sem_inc(consts, 1)
                elif name == "deg":
                    link(dve.tensor_reduce(deg[:], A, AX.X, ALU.add))
                    dve.tensor_scalar(deg_on[:], deg[:], 0.0, None, ALU.is_gt)
                    dve.tensor_scalar(deg_lo[:], deg[:], TINY, None, ALU.max)
                    link(dve.tensor_scalar(betaI[:], ident, beta_c, None, ALU.mult))
                    dve.sem_inc(consts, 1)
                elif name == "adn":
                    dve.wait_ge(deg_pow, 1)
                    link(dve.tensor_tensor(dis[:], deg_p[:], deg_on[:], ALU.mult))
                    dve.tensor_scalar(adn[:], A, dis[:], None, ALU.mult).then_inc(consts, 1)
                elif name == "NT":
                    dve.wait_ge(adn_turned, 1)
                    dve.tensor_scalar(NT[:], bank[NS - 1][0][:, 0, 0:P], dis[:], None, ALU.mult).then_inc(consts, 1)
                elif name == "Z":
                    both(w3s, "w3")
                    halves("Z", w3s[:])
                elif name == "V":
                    both(w5s, "w5")
                    halves("V", w5s[:])
                elif name == "gate_bias":
                    dve.tensor_tensor(gate_sum[:, 2, :], gate_raw[:, 2, :], gate_raw[:, 4, :], ALU.add)
                    link(dve.tensor_tensor(gate_sum[:, 0:2, :], gate_raw[:, 0:2, :],
                                           gate_raw[:, 3:4, :].broadcast_to([P, 2, KB]), ALU.add))
                    link(dve.tensor_scalar(gate_bias[:, 0:2, :], gate_sum[:, 0:2, :], 0.5, None, ALU.mult))
                    dve.tensor_copy(gate_bias[:, 2, :], gate_sum[:, 2, :]).then_inc(consts, 1)
                elif name == "R":
                    both(w4s, "w4")
                    link(dve.tensor_tensor(w43[:], w4s[:], w3s[:], ALU.subtract))
                    halves("R", w43[:])
                elif name == "UC":
                    link(dve.tensor_scalar(u5h[:], raw["u5"][:], 0.5, None, ALU.mult))
                    halves("UC", u5h[:])
                else:
                    halves(name, raw[load_of[name]][:])

            def stats_of(s, g, layer):
                src = X[s] if layer == 0 else RES[s]
                if layer == 0:
                    dve.wait_ge(x_in.sem[s], x_in.count(g, 16))
                else:
                    dve.wait_ge(res.sem[s], res.count(g, layer))
                for b in range(GB):
                    ins = dve.bn_stats(stats[s][:, b, :], src[:, b, :])
                ins.then_inc(ln_mv.sem[s], 1)

            def aggregate(s, g, layer):
                dve.wait_ge(ln_mv.sem[s], ln_mv.count(g, 3 * layer + 1))
                dve.sem_inc(ln_mv.sem[s], 1)
                for b in range(GB):
                    ins = dve.bn_aggr(mv[s][:, b, :], stats[s][:, b, :])
                ins.then_inc(ln_mv.sem[s], 1)

            def by_graph(ap):
                return ap.rearrange("p (b m) -> p b m", m=P)

            def wide(col):
                return col[:].rearrange("p (b o) -> p b o", o=1).broadcast_to([P, GB, P])

            def soft_step(ins, s, g, n):
                ins.then_inc(soft.sem[s], 1)
                dve.wait_ge(soft.sem[s], soft.count(g, n))

            def node_scores(s, g):
                dve.wait_ge(h_ready.sem[s], h_ready.count(g, 1))
                for score, n, products in ((s2, 1, E1), (s1, 0, E2)):
                    for b in range(GB):
                        ins = dve.tensor_tensor_reduce(out=products[s][:, b, :], in0=H[s][:, b, :],
                                                       in1=W0a[:, n, :], scale=1.0, scalar=0.0, op0=ALU.mult,
                                                       op1=ALU.add, accum_out=score[s][:, b:b + 1])
                    ins.then_inc(soft.sem[s], 1)

            def exponents(s, g):
                e1, e2 = by_graph(E1[s][:, 0, :]), by_graph(E2[s][:, 0, :])
                dve.wait_ge(soft.sem[s], soft.count(g, 2))
                dve.wait_ge(in_bank0.sem[s], in_bank0.count(g, "s2_rows"))
                soft_step(dve.tensor_tensor(e1, by_graph(bank[s][0][:, 0, :]), wide(s1[s]), ALU.add), s, g, 3)
                soft_step(dve.scalar_tensor_tensor(e2, e1, SLOPE, e1, ALU.mult, ALU.max), s, g, 4)
                soft_step(dve.tensor_tensor(e1, e2, A.rearrange("p (o m) -> p o m", o=1)
                                            .broadcast_to([P, GB, P]), ALU.mult), s, g, 5)
                soft_step(dve.tensor_reduce(top[s][:], e1, AX.X, ALU.max), s, g, 6)
                dve.tensor_tensor(e2, e1, wide(top[s]), ALU.subtract).then_inc(soft.sem[s], 1)

            def probabilities(s, g):
                dve.wait_ge(p_exp.sem[s], p_exp.count(g, 1))
                soft_step(dve.tensor_reduce(tot[s][:], by_graph(E1[s][:, 0, :]), AX.X, ALU.add), s, g, 8)
                soft_step(dve.reciprocal(rtot[s][:], tot[s][:]), s, g, 9)
                for b in range(GB):
                    ins = dve.scalar_tensor_tensor(E2[s][:, 0, b * P:(b + 1) * P], E1[s][:, 0, b * P:(b + 1) * P],
                                                   rtot[s][:, b:b + 1], betaI[:], ALU.mult, ALU.add)
                ins.then_inc(p_beta.sem[s], 1)

            def elu(s, g):
                dve.wait_ge(elu_e.sem[s], elu_e.count(g, 1))
                dve.tensor_scalar(E2[s][:], E1[s][:], 1.0, -1.0, ALU.min, ALU.add).then_inc(elu_v.sem[s], 1)
                dve.wait_ge(elu_v.sem[s], elu_v.count(g, 1))
                dve.tensor_tensor(E1[s][:], bank[s][1][:], E2[s][:], ALU.max).then_inc(elu_v.sem[s], 1)
                dve.wait_ge(elu_v.sem[s], elu_v.count(g, 2))
                dve.tensor_tensor(RES[s][:], E1[s][:], X[s][:], ALU.add).then_inc(res.sem[s], 1)

            def low(s, g, out, whole, high, led, n, done):
                dve.wait_ge(led.sem[s], led.count(g, n))
                dve.tensor_tensor(out, whole, high.bitcast(F32), ALU.subtract).then_inc(done.sem[s], 1)

            def do(part, s, g):
                kind, n = kind_of(part)
                if kind == "stats":
                    stats_of(s, g, n)
                elif kind == "aggr":
                    aggregate(s, g, n)
                elif part == "node":
                    node_scores(s, g)
                elif part == "soft_a":
                    exponents(s, g)
                elif part == "soft_b":
                    probabilities(s, g)
                elif part == "elu":
                    elu(s, g)
                elif kind == "y_lo":
                    low(s, g, Al[s][:], bank[s][0][:], Ah[s][:], a_hi, f"spread{n}", a_lo)
                elif part == "x2":
                    dve.wait_ge(rb.sem[s], rb.count(g, 1))
                    dve.wait_ge(in_bank1.sem[s], in_bank1.count(g, "mix1"))
                    dve.tensor_tensor(RES[s][:], bank[s][1][:], RB[s][:], ALU.add).then_inc(res.sem[s], 1)
                elif part == "out":
                    dve.wait_ge(rb.sem[s], rb.count(g, 2))
                    dve.wait_ge(stored.sem[s], stored.count(g, 16))
                    dve.wait_ge(in_bank1.sem[s], in_bank1.count(g, "mix3"))
                    dve.tensor_tensor(OUT[s][:], bank[s][1][:], RB[s][:], ALU.add).then_inc(out_ready.sem[s], 1)
                elif kind == "h_lo":
                    low(s, g, HTl[s][:], HT[s][:], HTh[s][:], hT_hi, n + 1, hT_lo)
                elif kind == "a_lo":
                    low(s, g, Al[s][:], bank[s][1][:], Ah[s][:], a_hi, f"a{n}", a_lo)
                elif kind == "q":
                    dve.wait_ge(r_ready.sem[s], r_ready.count(g, n + 1))
                    dve.scalar_tensor_tensor(QT[s][:], TR[s][:], 1.0, HT[s][:], ALU.add, ALU.mult)\
                       .then_inc(q_ready.sem[s], 1)
                elif kind == "q_lo":
                    low(s, g, QTl[s][:], QT[s][:], QTh[s][:], q_hi, f"r{n}", q_lo)
                elif kind == "upd":
                    dve.wait_ge(c_ready.sem[s], c_ready.count(g, n + 1))
                    dve.tensor_tensor(QT[s][:], HV[s][:], HT[s][:], ALU.subtract).then_inc(upd.sem[s], 1)
                    dve.wait_ge(upd.sem[s], upd.count(g, 2 * n + 1))
                    dve.scalar_tensor_tensor(HV[s][:], TZ[s][:], 1.0, QT[s][:], ALU.add, ALU.mult)\
                       .then_inc(upd.sem[s], 1)
                    dve.wait_ge(upd.sem[s], upd.count(g, 2 * n + 2))
                    dve.scalar_tensor_tensor(HT[s][:], HV[s][:], 0.5, HT[s][:], ALU.mult, ALU.add)\
                       .then_inc(hT_ready.sem[s], 1)
                elif part == "x3":
                    dve.wait_ge(in_bank1.sem[s], in_bank1.count(g, f"back{T}"))
                    dve.tensor_tensor(RES[s][:], bank[s][1][:], RES[s][:], ALU.add).then_inc(res.sem[s], 1)
                elif part in CONSTS:
                    constant(part)

            walk(dve, DVE_START, DVE_STEADY, DVE_END, do)

        @block.tensor
        def _(pe):
            awaited = Awaited()
            needs = {"mix0": "W0", "spread1": "NT", "mix1": "W1", "u0": "U", "z0": "Z", "v0": "V", "r0": "R",
                     "c0": "UC", "mix3": "WL"}

            def back(s, done):
                for b in range(GB):
                    for k in range(KB):
                        ins = pe.transpose(bank[s][1][:, b, k * P:(k + 1) * P], HT[s][:, k, b * P:(b + 1) * P], ident)
                ins.then_inc(done.sem[s], 1)

            def spread(s, to, right, done):
                for k in range(KB):
                    for b in range(GB):
                        ins = pe.matmul(bank[s][to][:, k, b * P:(b + 1) * P], H[s][:, b, k * P:(k + 1) * P],
                                        right(b), start=True, stop=True)
                ins.then_inc(done.sem[s], 1)

            def rows(s, g, left_hi, left_lo, key, low_ready, low_n, done):
                for n, (left, wk) in enumerate(((left_hi, hi), (left_hi, lo), (left_lo, hi))):
                    if left is left_lo:
                        pe.wait_ge(low_ready.sem[s], low_ready.count(g, low_n))
                    for b in range(GB):
                        for k in range(KB):
                            ins = pe.matmul(bank[s][1][:, b, :], left[s][:, k, b * P:(b + 1) * P], wk[key][:, k, :],
                                            start=(n == b == k == 0), stop=(n == 2 and k == KB - 1),
                                            skip_group_check=True)
                ins.then_inc(done.sem[s], 1)

            def gate(s, g, key, right_hi, right_lo, to, opens, closes, low_ready, low_n, done):
                for n, (wk, right) in enumerate(((hi, right_hi), (lo, right_hi), (hi, right_lo))):
                    if right is right_lo:
                        pe.wait_ge(low_ready.sem[s], low_ready.count(g, low_n))
                    for o in range(KB):
                        for k in range(KB):
                            ins = pe.matmul(bank[s][to][:, o, :], wk[key][:, k, o * P:(o + 1) * P], right[s][:, k, :],
                                            start=(opens and n == o == k == 0),
                                            stop=(closes and n == 2 and k == KB - 1), skip_group_check=True)
                if done is not None:
                    ins.then_inc(done.sem[s], 1)

            def do(part, s, g):
                kind, n = kind_of(part)
                if part in needs and awaited.new(needs[part]):
                    pe.wait_ge(consts, made(needs[part]))
                if part == "w0a_sum":
                    pe.wait_ge(loaded["w0T"], 16)
                    pe.wait_ge(consts, made("a_bc"))
                    for n in range(2):
                        for k in range(KB):
                            ins = pe.matmul(bank[NS - 1][1][:, n, :], a_bc[:, n * KB + k, :], W0T[:, k, :],
                                            start=(k == 0), stop=(k == KB - 1))
                    ins.then_inc(w0a_sum, 1)
                elif part == "turn_adn":
                    pe.wait_ge(consts, made("adn"))
                    pe.transpose(bank[NS - 1][0][:, 0, 0:P], adn[:], ident).then_inc(adn_turned, 1)
                elif part == "s2_rows":
                    pe.wait_ge(soft.sem[s], soft.count(g, 1))
                    for b in range(GB):
                        ins = pe.transpose(bank[s][0][:, 0, b * P:(b + 1) * P],
                                           s2[s][:, b:b + 1].broadcast_to([P, P]), ident)
                    ins.then_inc(in_bank0.sem[s], 1)
                elif part == "turn_p":
                    pe.wait_ge(p_beta.sem[s], p_beta.count(g, 1))
                    for b in range(GB):
                        ins = pe.transpose(bank[s][0][:, 0, b * P:(b + 1) * P], E2[s][:, 0, b * P:(b + 1) * P], ident)
                    ins.then_inc(in_bank0.sem[s], 1)
                elif part == "spread0":
                    pe.wait_ge(pt_ready.sem[s], pt_ready.count(g, 1))
                    spread(s, 0, lambda b: PT[s][:, 0, b * P:(b + 1) * P], in_bank0)
                elif kind == "spread":
                    pe.wait_ge(h_ready.sem[s], h_ready.count(g, 2 if n == 1 else 4))
                    spread(s, 0, lambda b: NT[:] if n == 1 else AT, in_bank0)
                elif kind == "mix":
                    pe.wait_ge(a_hi.sem[s], a_hi.count(g, f"spread{n}"))
                    rows(s, g, Ah, Al, {0: "W0", 1: "W1", 3: "WL"}[n], a_lo, f"spread{n}", in_bank1)
                elif part == "turn2":
                    pe.wait_ge(h_ready.sem[s], h_ready.count(g, 3))
                    for k in range(KB):
                        for b in range(GB):
                            ins = pe.transpose(bank[s][0][:, k, b * P:(b + 1) * P],
                                               H[s][:, b, k * P:(k + 1) * P], ident)
                    ins.then_inc(in_bank0.sem[s], 1)
                elif kind == "back":
                    pe.wait_ge(hT_ready.sem[s], hT_ready.count(g, 1 + n))
                    back(s, in_bank1)
                elif kind == "u":
                    pe.wait_ge(hT_hi.sem[s], hT_hi.count(g, n + 1))
                    gate(s, g, "U", HTh, HTl, 0, True, False, hT_lo, n + 1, None)
                elif kind == "a":
                    if n:
                        pe.wait_ge(h_back.sem[s], h_back.count(g, n))
                    else:
                        pe.wait_ge(h_ready.sem[s], h_ready.count(g, 3))
                    spread(s, 1, lambda b: AT, in_bank1)
                elif kind == "z":
                    pe.wait_ge(a_hi.sem[s], a_hi.count(g, f"a{n}"))
                    gate(s, g, "Z", Ah, Al, 0, False, True, a_lo, f"a{n}", in_bank0)
                elif kind == "v":
                    gate(s, g, "V", Ah, Al, 1, True, False, a_lo, f"a{n}", None)
                elif kind == "r":
                    pe.wait_ge(z_ready.sem[s], z_ready.count(g, n + 1))
                    gate(s, g, "R", Ah, Al, 0, False, True, a_lo, f"a{n}", in_bank0)
                elif kind == "c":
                    pe.wait_ge(q_hi.sem[s], q_hi.count(g, f"r{n}"))
                    gate(s, g, "UC", QTh, QTl, 1, False, True, q_lo, f"r{n}", in_bank1)

            walk(pe, PE_START, PE_STEADY, PE_END, do)


def kernel(x, adj, L0_gnn_W, L0_gnn_a, L0_gnn_beta, L1_gnn_weight, L1_gnn_bias, L2_gnn_w3_w, L2_gnn_w3_b,
           L2_gnn_u3_w, L2_gnn_u3_b, L2_gnn_w4_w, L2_gnn_w4_b, L2_gnn_w5_w, L2_gnn_w5_b, L2_gnn_u5_w,
           L2_gnn_u5_b, L3_gnn_weight, L3_gnn_bias):
    import numpy as np
    import concourse.bacc as bacc
    from concourse.bass_utils import run_bass_kernel_spmd

    def rows(v):
        return np.broadcast_to(np.asarray(v)[None, :], (P, C))

    def blocks(v):
        return np.asarray(v).reshape(-1, P).T

    adj, a = np.asarray(adj), np.asarray(L0_gnn_a)[:, 0]
    small = {"ident": np.eye(P, dtype=np.float32), "adj": adj, "adjT": adj.T, "a": blocks(a),
             "beta": np.broadcast_to(np.asarray(L0_gnn_beta)[None, :], (P, 1)),
             "gate_bias": np.concatenate([blocks(v) for v in (L2_gnn_w3_b, L2_gnn_w4_b, L2_gnn_w5_b, L2_gnn_u3_b,
                                                              L2_gnn_u5_b)], axis=1)}
    row = {"b1": rows(L1_gnn_bias), "bl": rows(L3_gnn_bias)}
    host = {
        "x": x,
        "small": np.concatenate([small[k] for k in SMALL], axis=1),
        "rows": np.concatenate([row[k] for k in ROWS], axis=1),
        "w0": L0_gnn_W,
        "w0T": np.asarray(L0_gnn_W).T,
        "w1": L1_gnn_weight,
        "w3T": np.asarray(L2_gnn_w3_w).T,
        "w4T": np.asarray(L2_gnn_w4_w).T,
        "w5T": np.asarray(L2_gnn_w5_w).T,
        "u3T": np.asarray(L2_gnn_u3_w).T,
        "u5T": np.asarray(L2_gnn_u5_w).T,
        "wl": L3_gnn_weight,
    }
    host = {k: np.ascontiguousarray(v) for k, v in host.items()}
    nc = bacc.Bacc("TRN2", target_bir_lowering=False, num_devices=1)
    args = [nc.dram_tensor(k + "_dram", v.shape, mybir.dt.from_np(v.dtype), kind="ExternalInput").ap()
            for k, v in host.items()]
    args.append(nc.dram_tensor("out_dram", (B, P, C), F32, kind="ExternalOutput").ap())
    build(nc, *args)
    r = run_bass_kernel_spmd(nc, [{k + "_dram": v for k, v in host.items()}], core_ids=[0])
    return r.results[0]["out_dram"]
```
